# Optimizing a Trainium2 kernel written in Bass

```python
import numpy as np
import jax
import jax.numpy as jnp

def _softmax(x, axis=-1):
    return jax.nn.softmax(x, axis=axis)

def _gelu(x):
    return jax.nn.gelu(x, approximate=True)

def _silu(x):
    return jax.nn.silu(x)

def _sigmoid(x):
    return jax.nn.sigmoid(x)

def _layernorm(x, axis=-1, eps=1e-05):
    m = jnp.mean(x, axis=axis, keepdims=True)
    v = jnp.var(x, axis=axis, keepdims=True)
    return (x - m) / jnp.sqrt(v + eps)

def _scatter_add(tgt, idx, src, axis=0):
    return tgt.at[idx].add(src)

def _segment_sum(src, seg, n):
    return jax.ops.segment_sum(src, seg, n)
kernel_name = 'mk_adj_preln_d1_adj_r2_a31870'

def setup_inputs(seed: int=0):
    np.random.seed(seed)
    _w = jnp.asarray

    def _rec_inputs():
        import jax
        import jax.numpy as jnp
        _gk = jax.random.key(seed)
        x = -0.001547 + 1.001 * jax.random.normal(jax.random.fold_in(_gk, 1), (1354, 64), jnp.float32)
        _w = (1.0 + jnp.arange(1354, dtype=jnp.float32)) ** (-0.5)
        _w = _w / _w.mean()
        _pij = jnp.clip(0.0118168 * _w[:, None] * _w[None, :], 0.0, 1.0)
        _a = jax.random.uniform(jax.random.fold_in(_gk, 2), (1354, 1354)) < _pij
        _a = jnp.logical_or(_a, jnp.eye(1354, dtype=bool))
        _af = _a.astype(jnp.float32)
        _af = _af * jax.random.uniform(jax.random.fold_in(_gk, 3), (1354, 1354), jnp.float32, 0.05, 1)
        adj = _af
        return (x, adj)
    x, adj = _rec_inputs()

    def _L0_gnn_setup():
        import jax, jax.numpy as jnp
        import numpy as np

        def _laplacian(A):
            d = jnp.sum(A, axis=-1)
            dinv = 1.0 / jnp.sqrt(d)
            return A * dinv[:, None] * dinv[None, :]

        def _poly(A, theta):
            t = jax.nn.sigmoid(theta)
            N = A.shape[-1]
            P = jnp.eye(N, dtype=A.dtype)
            seg = P
            for i in range(theta.shape[0]):
                seg = seg @ A
                P = P + seg * t[i]
            return P
        key = jax.random.key(seed)
        k1, k2, k3, k4 = jax.random.split(key, 4)
        N, DIN, DOUT, K_CHEB = (2048, 64, 64, 2)
        return {'x': jax.random.normal(k1, (N, DIN), dtype=jnp.float32), 'A': jax.random.uniform(k2, (N, N), dtype=jnp.float32), 'theta': jax.random.normal(k3, (K_CHEB,), dtype=jnp.float32), 'W': jax.random.normal(k4, (DOUT, DIN), dtype=jnp.float32) / np.float32(np.sqrt(DIN)), 'b': jnp.zeros((DOUT,), dtype=jnp.float32), 'k': 4}
    _L0_gnn_all = _L0_gnn_setup()
    _L0_gnn_in = {k: v for k, v in _L0_gnn_all.items() if k in ('theta', 'W', 'b')}
    del _L0_gnn_all
    return {'x': x, 'adj': adj, 'L0_gnn_theta': _L0_gnn_in['theta'], 'L0_gnn_W': _L0_gnn_in['W'], 'L0_gnn_b': _L0_gnn_in['b']}

def reference(x, adj, L0_gnn_theta, L0_gnn_W, L0_gnn_b):
    import jax
    import jax.numpy as jnp

    def _L0_gnn_ref(x, A, theta, W, b, k):
        import jax, jax.numpy as jnp
        import numpy as np

        def _laplacian(A):
            d = jnp.sum(A, axis=-1)
            dinv = 1.0 / jnp.sqrt(d)
            return A * dinv[:, None] * dinv[None, :]

        def _poly(A, theta):
            t = jax.nn.sigmoid(theta)
            N = A.shape[-1]
            P = jnp.eye(N, dtype=A.dtype)
            seg = P
            for i in range(theta.shape[0]):
                seg = seg @ A
                P = P + seg * t[i]
            return P
        S = _laplacian(A)
        S = _poly(S, theta)
        S = _laplacian(S)
        rank = jnp.argsort(jnp.argsort(-S, axis=-1), axis=-1)
        mask = jnp.where(rank < k, jnp.float32(1.0), jnp.float32(0.0))
        S = S * mask
        x = S @ x
        return x @ W.T + b
    h = jnp.maximum(_layernorm(x, axis=-1), 0.0)
    x = x + _L0_gnn_ref(h, adj, L0_gnn_theta, L0_gnn_W, L0_gnn_b, 4)
    return x

_drawn_inputs = setup_inputs


def setup_inputs(seed=0):
    import zlib

    import numpy as np

    out = dict(_drawn_inputs(seed))
    spreads = {'L0_gnn_b': (0.0, 0.1)}
    factors = {'L0_gnn_theta': 64.0}
    for name, (base, spread) in spreads.items():
        noise = np.random.default_rng([zlib.crc32(name.encode()), seed]).standard_normal(out[name].shape)
        drawn = base * np.exp(spread * noise) if base else spread * noise
        out[name] = jnp.asarray(drawn.astype(out[name].dtype))
    for name, factor in factors.items():
        out[name] = (out[name] * factor).astype(out[name].dtype)
    return out
```

```python
from contextlib import ExitStack

import concourse.bass as bass
from concourse import mybir


def poly_graph_kernel(nc, x, adj, theta, W, b, out):
    f32, f32r, bf16, u32 = mybir.dt.float32, mybir.dt.float32r, mybir.dt.bfloat16, mybir.dt.uint32
    ALU, ACT, AX = mybir.AluOpType, mybir.ActivationFunctionType, mybir.AxisListType

    P = 128
    N, F = x.shape
    FULL = N // P
    NT = FULL + 1
    LAST = N - FULL * P
    NP = NT * P
    KEEP = 4
    EPS = 1e-5
    CH = [(c, min(c + 512, N)) for c in range(0, N, 512)]
    BLK = [range(c, min(c + 4, NT)) for c in range(0, NT, 4)]
    NC = len(BLK)
    RING = 3
    XR = 3
    HEAD = 2

    def rows(k):
        return P if k < FULL else LAST

    ctx = ExitStack()
    with ctx:
        def sb(name, shape, dt=f32):
            return ctx.enter_context(nc.sbuf_tensor(name, shape, dt))

        def sem(name):
            return ctx.enter_context(nc.semaphore(name))

        A_hi = sb("A_hi", [P, NT, N], f32r)
        A_lo = sb("A_lo", [P, NT, N], f32r)
        L_hi = sb("L_hi", [P, 2, NP], f32r)
        L_lo = sb("L_lo", [P, 2, NP], f32r)
        LT = sb("LT", [P, NP])
        row_stage = sb("row_stage", [P, 2, N])
        stream = sb("stream", [P, RING, N])
        prod = sb("prod", [P, XR, N])
        V = sb("V", [P, NP])
        vec_bc = sb("vec_bc", [P, N])
        y_out = sb("y_out", [P, NT, F])
        ident = sb("ident", [P, P])
        t0_ident = sb("t0_ident", [P, P])
        gathered = sb("gathered", [P, KEEP, F])
        W_sb = sb("W_sb", [F, F])
        WT_sb = sb("WT_sb", [F, F])
        b_bc = sb("b_bc", [P, F])
        th = sb("th", [P, 2])
        t = sb("t", [P, 2])
        vec32 = sb("vec32", [P, 32])
        vec32T = sb("vec32T", [P, 32])
        deg = sb("deg", [P, NT])
        rdeg = sb("rdeg", [P, NT])
        s = sb("s", [P, NT])
        D = sb("D", [P, NT])
        yv = sb("yv", [P, NT])
        zv = sb("zv", [P, NT])
        deg2 = sb("deg2", [P, NT])
        w = sb("w", [P, NT])
        diag = sb("diag", [P, NT])
        c_col = sb("c_col", [P, NT])
        tmp = sb("tmp", [P, NT])
        mean = sb("mean", [P, NT])
        rstd = sb("rstd", [P, NT])
        top = sb("top", [P, 8])
        top2 = sb("top2", [P, 16])
        weight = sb("weight", [P, KEEP])
        index = sb("index", [P, 8], u32)
        xc = V[:, 0:NT * F].rearrange("p (k f) -> p k f", f=F)
        h = V[:, NT * F:2 * NT * F].rearrange("p (k f) -> p k f", f=F)
        prod_flat = prod[:, :, :].rearrange("p a n -> p (a n)")
        hT = prod_flat[0:F, 0:NP]
        g_sb = prod_flat[:, NP:NP + NT * F].rearrange("p (k f) -> p k f", f=F)
        act_junk = prod[:, 2, :]
        head_LT = LT[:, 0:8 * P].rearrange("p (a m q) -> p a m q", m=2, q=P)

        U = [ctx.enter_context(nc.psum_tensor(f"U{i}", [P, 3 * 512], f32)) for i in range(2)]
        T = ctx.enter_context(nc.psum_tensor("T", [P, 2, 512], f32))
        hT_ps = U[0][0:F, 0:NP]
        WT_ps = U[1][0:F, 1024:1024 + F]
        g_ps = U[1][:, 0:NT * F].rearrange("p (k f) -> p k f", f=F)

        g_dram = nc.dram_tensor("g_scratch", [N, F], f32).ap()
        vec_dram = nc.dram_tensor("vec_scratch", [NP], f32).ap()
        vec_cells = vec_dram.rearrange("(k b q) -> b k q", b=4, q=32)

        stage_in = [sem(f"stage_in{i}") for i in range(2)]
        stream_in = [sem(f"stream_in{i}") for i in range(RING)]
        x_in, small_in = sem("x_in"), sem("small_in")
        x_padded = sem("x_padded")
        ident_zero, ident_ready = sem("ident_zero"), sem("ident_ready")
        cleared = sem("cleared")
        th_exp, t_part, t_ready, t0i_ready = sem("th_exp"), sem("t_part"), sem("t_ready"), sem("t0i_ready")
        ln_step, ln_sqrt_in, ln_sqrt, h_ready = sem("ln_step"), sem("ln_sqrt_in"), sem("ln_sqrt"), sem("h_ready")
        hT_made, hT_copied, g_made, g_copied, g_stored = (
            sem("hT_made"), sem("hT_copied"), sem("g_made"), sem("g_copied"), sem("g_stored"))
        xb_ready = sem("xb_ready")
        deg_ready, rdeg_ready, s_ready = sem("deg_ready"), sem("rdeg_ready"), sem("s_ready")
        hi_ready, lo_ready = sem("hi_ready"), sem("lo_ready")
        T_made, T_used = sem("T_made"), sem("T_used")
        hd_scaled, hd_diag, hd_Lhi, hd_Llo = sem("hd_scaled"), sem("hd_diag"), sem("hd_Lhi"), sem("hd_Llo")
        LT_cleared = sem("LT_cleared")
        LT_scaled, LT_ready, Lhi_ready, Llo_ready = (
            sem("LT_scaled"), sem("LT_ready"), sem("Lhi_ready"), sem("Llo_ready"))
        U_done, U_copied, tail_chunk = sem("U_done"), sem("U_copied"), sem("tail_chunk")
        rs_in, rs_sqrt, rs_step = sem("rs_in"), sem("rs_sqrt"), sem("rs_step")
        vec_col, vec_turned, vec_stored, vec_in = sem("vec_col"), sem("vec_turned"), sem("vec_stored"), sem("vec_in")
        mv_done = sem("mv_done")
        V_scaled, V_ready, top_ready, index_ready, weight_ready = (
            sem("V_scaled"), sem("V_ready"), sem("top_ready"), sem("index_ready"), sem("weight_ready"))
        gather_begun, gather_in, term_added = sem("gather_begun"), sem("gather_in"), sem("term_added")
        out_stored = sem("out_stored")

        def T_count(m, c):
            return 3 * m + c - 2

        streamed = list(range(HEAD, NT)) + list(range(NT)) * 2
        MV1 = NT - HEAD
        MV2 = MV1 + NT

        block = ctx.enter_context(nc.Block())

        @block.sync
        def _(sp):
            def load_stage(m):
                sp.dma_start(row_stage[0:rows(m), m % 2, :],
                             adj[m * P:m * P + rows(m), :]).then_inc(stage_in[m % 2], 16)

            def load_stream(n):
                k = streamed[n]
                if n >= RING:
                    old = n - RING
                    if old < MV1:
                        sp.wait_ge(lo_ready, streamed[old] + 1)
                    else:
                        sp.wait_ge(mv_done, old - MV1 + 1)
                sp.dma_start(stream[0:rows(k), n % RING, :],
                             adj[k * P:k * P + rows(k), :]).then_inc(stream_in[n % RING], 16)

            def broadcast_vector(v):
                sp.wait_ge(vec_turned, v + 1)
                for q in range(4):
                    sp.dma_start(vec_cells[q], vec32T[32 * q:32 * q + NT, :]).then_inc(vec_stored, 16)
                sp.wait_ge(vec_stored, 64 * (v + 1))
                sp.dma_start(vec_bc[:, :], vec_dram[0:N].partition_broadcast(P)).then_inc(vec_in, 16)

            load_stage(0)
            load_stage(1)
            for n in range(MV1):
                load_stream(n)
            for n in range(MV1, MV1 + RING):
                load_stream(n)
            broadcast_vector(0)
            sp.wait_ge(lo_ready, HEAD)
            sp.wait_ge(T_made, NC)
            load_stage(2)
            load_stage(3)
            for n in range(MV1 + RING, MV2 + RING):
                load_stream(n)
                if n == MV2:
                    sp.wait_ge(T_made, T_count(2, NC - 1))
                    load_stage(4)
            broadcast_vector(1)
            for n in range(MV2 + RING, len(streamed)):
                load_stream(n)
                if n == MV2 + RING + 2:
                    sp.wait_ge(T_made, T_count(3, NC - 1))
                    load_stage(5)
            broadcast_vector(2)
            with sp.Fori(3, FULL // 2) as pair:
                for i in range(2):
                    sp.wait_ge(T_made, 6 * pair + 3 * (i - 2))
                    sp.dma_start(row_stage[:, i, :],
                                 adj[bass.ds((2 * pair + i) * P, P), :]).then_inc(stage_in[i], 16)
            sp.wait_ge(T_made, T_count(FULL - 2, NC - 1))
            load_stage(FULL)
            sp.wait_ge(term_added, KEEP * FULL)
            sp.dma_start(out[0:FULL * P, :].rearrange("(k p) f -> p k f", p=P),
                         y_out[:, 0:FULL, :]).then_inc(out_stored, 16)
            sp.wait_ge(term_added, KEEP * NT)
            sp.dma_start(out[FULL * P:N, :], y_out[0:LAST, FULL, :]).then_inc(out_stored, 16)
            sp.wait_ge(out_stored, 32)

        @block.gpsimd
        def _(pool):
            nc.gpsimd.memset(y_out[:, FULL, :], 0.0).then_inc(x_padded, 1)
            nc.gpsimd.memset(ident[:, :], 0.0).then_inc(ident_zero, 1)
            pool.wait_ge(ident_zero, 1)
            nc.gpsimd.affine_select(out=ident[:, :], in_=ident[:, :], compare_op=ALU.not_equal, fill=1.0,
                                    base=0, pattern=[[-1, P]], channel_multiplier=1).then_inc(ident_ready, 1)
            pool.wait_ge(g_copied, 1)
            pool.dma_start(g_dram[0:FULL * P, :].rearrange("(k p) f -> p k f", p=P),
                           g_sb[:, 0:FULL, :]).then_inc(g_stored, 16)
            pool.dma_start(g_dram[FULL * P:N, :], g_sb[0:LAST, FULL, :]).then_inc(g_stored, 16)
            pool.wait_ge(g_stored, 32)
            with pool.Fori(0, FULL) as r:
                pool.wait_ge(index_ready, r + 1)
                pool.sem_inc(gather_begun, 1)
                for j in range(KEEP):
                    nc.gpsimd.indirect_dma_start(
                        gathered[:, j, :], None, g_dram[:, :],
                        bass.IndirectOffsetOnAxis(ap=index[:, j:j + 1], axis=0)).then_inc(gather_in, 16)
            pool.wait_ge(index_ready, NT)
            for j in range(KEEP):
                nc.gpsimd.indirect_dma_start(
                    gathered[0:LAST, j, :], None, g_dram[:, :],
                    bass.IndirectOffsetOnAxis(ap=index[0:LAST, j:j + 1], axis=0)).then_inc(gather_in, 16)

        @block.scalar
        def _(act):
            act.wait_ge(x_padded, 1)
            act.dma_start(y_out[:, 0:FULL, :], x[0:FULL * P, :].rearrange("(k p) f -> p k f", p=P)).then_inc(x_in, 16)
            act.dma_start(y_out[0:LAST, FULL, :], x[FULL * P:N, :]).then_inc(x_in, 16)
            act.dma_start(th[:, :], theta.partition_broadcast(P)).then_inc(small_in, 16)
            act.dma_start(b_bc[:, :], b.partition_broadcast(P)).then_inc(small_in, 16)
            act.dma_start(W_sb[:, :], W).then_inc(small_in, 16)
            act.wait_ge(small_in, 48)
            nc.scalar.activation(t[:, :], th[:, :], ACT.Exp, scale=-1.0).then_inc(th_exp, 1)
            act.wait_ge(ln_sqrt_in, 1)
            nc.scalar.activation(rstd[:, :], mean[:, :], ACT.Sqrt).then_inc(ln_sqrt, 1)
            act.wait_ge(hT_made, 1)
            nc.scalar.activation(hT, hT_ps, ACT.Copy).then_inc(hT_copied, 1)

            def row_sum(k):
                if k < HEAD:
                    act.wait_ge(stage_in[k], 16)
                    src = row_stage[:, k, :]
                else:
                    n = k - HEAD
                    act.wait_ge(stream_in[n % RING], 16 * (n // RING + 1))
                    src = stream[0:rows(k), n % RING, :]
                if k:
                    act.wait_ge(deg_ready, k)
                nc.scalar.activation(act_junk[0:rows(k), :], src, ACT.Copy,
                                     accum_out=deg[0:rows(k), k:k + 1]).then_inc(deg_ready, 1)

            act.wait_ge(cleared, 1)
            row_sum(0)
            row_sum(1)
            for k in range(NT):
                kr = rows(k)
                if k % 4 == 0:
                    act.wait_ge(T_made, k // 4 + 1)
                act.wait_ge(s_ready, k + 1)
                if k >= 4:
                    act.wait_ge(hd_Llo, k - 3)
                scaled = nc.scalar.activation(head_LT[0:kr, k % 4, :, :],
                                              T[0:kr, :, (k % 4) * P:(k % 4 + 1) * P], ACT.Copy,
                                              scale=s[0:kr, k:k + 1])
                scaled.then_inc(hd_scaled, 1)
                if k + 2 < NT:
                    row_sum(k + 2)
                act.wait_ge(hd_scaled, k + 1)
                if k < HEAD:
                    act.wait_ge(hd_diag, k + 1)
                if k % 4 == 3 or k == NT - 1:
                    act.sem_inc(T_used, 1)
                nc.scalar.activation(L_hi[0:kr, :, k * P:(k + 1) * P], head_LT[0:kr, k % 4, :, :],
                                     ACT.Copy).then_inc(hd_Lhi, 1)
            act.wait_ge(rs_in, 1)
            nc.scalar.activation(D[:, :], deg[:, :], ACT.Sqrt).then_inc(rs_sqrt, 1)

            def transpose_scaled(m, p, bank0):
                for c in range(NC):
                    act.wait_ge(T_made, 3 * m + (c - 2))
                    for k in BLK[c]:
                        ins = nc.scalar.activation(LT[0:rows(k), k * P:(k + 1) * P],
                                                   T[0:rows(k), (bank0 + c) % 2, (k % 4) * P:(k % 4 + 1) * P],
                                                   ACT.Copy, scale=s[0:rows(k), k:k + 1])
                    ins.then_inc(T_used, 1)
                act.wait_ge(LT_ready, m - 1)
                nc.scalar.activation(L_hi[:, p, :], LT[:, :], ACT.Copy).then_inc(Lhi_ready, 1)

            def copy_product(m, p, slot):
                act.wait_ge(U_done, m + 1)
                nc.scalar.activation(prod[:, slot, :] if isinstance(slot, int) else
                                     prod_flat[:, bass.ds(slot * N, N)],
                                     U[p][:, 0:N], ACT.Copy).then_inc(U_copied, 1)

            act.wait_ge(LT_cleared, 1)
            act.wait_ge(U_done, 1)
            transpose_scaled(2, 0, 0)
            act.wait_ge(g_stored, 32)
            copy_product(0, 0, 0)
            for m in (2, 3):
                copy_product(m - 1, (m - 1) % 2, m - 1)
                act.wait_ge(Llo_ready, m - 1)
                transpose_scaled(m + 1, (m + 1) % 2, (m + 1) % 2)
            act.wait_ge(rs_in, 2)
            nc.scalar.activation(w[:, :], deg2[:, :], ACT.Sqrt).then_inc(rs_sqrt, 1)
            with act.Fori(2, FULL // 2) as pair:
                for i in range(2):
                    m = 2 * pair
                    act.wait_ge(V_scaled, m + (i - 3))
                    copy_product(m + (i - 1), (i + 1) % 2, (m + (i - 1)) % XR)
                    act.wait_ge(Llo_ready, m + (i - 1))
                    transpose_scaled(m + (i + 1), (i + 1) % 2, (i + 1) % 2)
            act.wait_ge(V_scaled, FULL - 3)
            copy_product(FULL - 1, 1, (FULL - 1) % XR)

        @block.vector
        def _(dve):
            v = nc.vector

            def rsqrt_newton(dst, src, step_sem, base):
                v.reciprocal(dst, dst).then_inc(step_sem, 1)
                dve.wait_ge(step_sem, base + 1)
                v.tensor_tensor(tmp[:, :], dst, dst, ALU.mult).then_inc(step_sem, 1)
                dve.wait_ge(step_sem, base + 2)
                v.tensor_tensor(tmp[:, :], tmp[:, :], src, ALU.mult).then_inc(step_sem, 1)
                dve.wait_ge(step_sem, base + 3)
                v.tensor_scalar(tmp[:, :], tmp[:, :], -0.5, 1.5, ALU.mult, ALU.add).then_inc(step_sem, 1)
                dve.wait_ge(step_sem, base + 4)
                v.tensor_tensor(dst, dst, tmp[:, :], ALU.mult).then_inc(step_sem, 1)
                dve.wait_ge(step_sem, base + 5)

            v.memset(vec32[:, :], 0.0)
            v.memset(yv[:, :], 0.0)
            v.memset(zv[:, :], 0.0)
            v.memset(deg[:, :], 1.0).then_inc(cleared, 1)

            dve.wait_ge(th_exp, 1)
            v.tensor_scalar_add(t[:, :], t[:, :], 1.0).then_inc(t_part, 1)
            dve.wait_ge(t_part, 1)
            v.reciprocal(t[:, :], t[:, :]).then_inc(t_ready, 1)
            dve.wait_ge(t_ready, 1)
            dve.wait_ge(ident_ready, 1)
            v.tensor_scalar(t0_ident[:, :], ident[:, :], t[:, 0:1], None, ALU.mult).then_inc(t0i_ready, 1)

            dve.wait_ge(x_in, 32)
            v.reduce_sum(mean[:, :], y_out[:, :, :], AX.X).then_inc(ln_step, 1)
            dve.wait_ge(ln_step, 1)
            v.tensor_scalar(mean[:, :], mean[:, :], 1.0 / F, None, ALU.mult).then_inc(ln_step, 1)
            dve.wait_ge(ln_step, 2)
            v.tensor_tensor(xc, y_out[:, :, :], mean[:, :].unsqueeze(2).to_broadcast([P, NT, F]),
                            ALU.subtract).then_inc(ln_step, 1)
            dve.wait_ge(ln_step, 3)
            v.tensor_tensor(h, xc, xc, ALU.mult).then_inc(ln_step, 1)
            dve.wait_ge(ln_step, 4)
            v.reduce_sum(mean[:, :], h, AX.X).then_inc(ln_step, 1)
            dve.wait_ge(ln_step, 5)
            v.tensor_scalar(mean[:, :], mean[:, :], 1.0 / F, EPS, ALU.mult, ALU.add).then_inc(ln_sqrt_in, 1)
            dve.wait_ge(ln_sqrt_in, 1)
            dve.wait_ge(ln_sqrt, 1)
            rsqrt_newton(rstd[:, :], mean[:, :], ln_step, 5)
            v.scalar_tensor_tensor(h, xc, 0.0, rstd[:, :].unsqueeze(2).to_broadcast([P, NT, F]),
                                   ALU.max, ALU.mult).then_inc(h_ready, 1)
            dve.wait_ge(small_in, 48)
            v.tensor_tensor(y_out[:, :, :], y_out[:, :, :], b_bc[:, :].unsqueeze(1).to_broadcast([P, NT, F]),
                            ALU.add).then_inc(xb_ready, 1)
            dve.wait_ge(hT_made, 1)
            v.tensor_copy(WT_sb[:, :], WT_ps).then_inc(hT_copied, 1)

            for k in range(NT):
                kr = rows(k)
                if k < HEAD:
                    dve.wait_ge(stage_in[k], 16)
                    src = row_stage[:, k, :]
                else:
                    n = k - HEAD
                    dve.wait_ge(stream_in[n % RING], 16 * (n // RING + 1))
                    src = stream[0:kr, n % RING, :]
                v.tensor_copy(A_hi[0:kr, k, :], src).then_inc(hi_ready, 1)
                dve.wait_ge(deg_ready, k + 1)
                v.reciprocal(rdeg[:, k:k + 1], deg[:, k:k + 1]).then_inc(rdeg_ready, 1)
                dve.wait_ge(rdeg_ready, k + 1)
                v.tensor_scalar(s[:, k:k + 1], rdeg[:, k:k + 1], t[:, 1:2], None, ALU.mult).then_inc(s_ready, 1)
                dve.wait_ge(hi_ready, k + 1)
                v.tensor_tensor(A_lo[0:kr, k, :], src, A_hi[0:kr, k, :].bitcast(f32),
                                ALU.subtract).then_inc(lo_ready, 1)
                if k == 1:
                    dve.wait_ge(g_made, 1)
                    v.tensor_copy(g_sb[:, :, :], g_ps).then_inc(g_copied, 1)
                if k < HEAD:
                    dve.wait_ge(hd_scaled, k + 1)
                    dve.wait_ge(t0i_ready, 1)
                    v.tensor_tensor(head_LT[:, k, k, :], head_LT[:, k, k, :], t0_ident[:, :],
                                    ALU.add).then_inc(hd_diag, 1)
                dve.wait_ge(hd_Lhi, k + 1)
                v.tensor_tensor(L_lo[0:kr, :, k * P:(k + 1) * P], head_LT[0:kr, k % 4, :, :],
                                L_hi[0:kr, :, k * P:(k + 1) * P].bitcast(f32), ALU.subtract).then_inc(hd_Llo, 1)
            dve.wait_ge(hd_Llo, NT)
            v.memset(LT[:, FULL * P:NP], 0.0).then_inc(LT_cleared, 1)

            v.tensor_scalar(deg[:, :], deg[:, :], 1.0, None, ALU.mult).then_inc(rs_in, 1)
            dve.wait_ge(rs_sqrt, 1)
            rsqrt_newton(D[:, :], deg[:, :], rs_step, 0)

            def turn_vector(n, col):
                v.tensor_copy(vec32[:, 0:NT], col).then_inc(vec_col, 1)
                dve.wait_ge(vec_col, n + 1)
                if n >= 1:
                    dve.wait_ge(vec_stored, 64 * n)
                v.transpose(vec32T[:, :], vec32[:, :]).then_inc(vec_turned, 1)

            def split_L(m, p):
                dve.wait_ge(T_used, 3 * m)
                v.tensor_tensor(LT[:, bass.ds(m * P, P)], LT[:, bass.ds(m * P, P)], t0_ident[:, :],
                                ALU.add).then_inc(LT_ready, 1)
                dve.wait_ge(Lhi_ready, m - 1)
                v.tensor_tensor(L_lo[:, p, :] if isinstance(p, int) else L_lo_flat[:, bass.ds(p * NP, NP)],
                                LT[:, :],
                                L_hi[:, p, :].bitcast(f32) if isinstance(p, int) else
                                L_hi_flat[:, bass.ds(p * NP, NP)].bitcast(f32),
                                ALU.subtract).then_inc(Llo_ready, 1)

            L_lo_flat = L_lo[:, :, :].rearrange("p a n -> p (a n)")
            L_hi_flat = L_hi[:, :, :].rearrange("p a n -> p (a n)")

            def times_vector(n, dst):
                for k in range(NT):
                    i = (MV1, MV2)[n] + k
                    dve.wait_ge(stream_in[i % RING], 16 * (i // RING + 1))
                    if NT * n + k:
                        dve.wait_ge(mv_done, NT * n + k)
                    v.tensor_tensor_reduce(out=V[0:rows(k), 0:N], in0=stream[0:rows(k), i % RING, :],
                                           in1=vec_bc[0:rows(k), :], scale=1.0, scalar=0.0,
                                           op0=ALU.mult, op1=ALU.add,
                                           accum_out=dst[0:rows(k), k:k + 1]).then_inc(mv_done, 1)
                dve.wait_ge(mv_done, NT * (n + 1))

            turn_vector(0, D[:, :])
            split_L(2, 0)
            dve.wait_ge(vec_in, 16)
            times_vector(0, yv)
            v.tensor_tensor(tmp[:, :], s[:, :], yv[:, :], ALU.mult).then_inc(rs_step, 1)
            dve.wait_ge(rs_step, 6)
            turn_vector(1, tmp[:, :])
            split_L(3, 1)
            dve.wait_ge(vec_in, 32)
            times_vector(1, zv)
            v.scalar_tensor_tensor(deg2[:, :], yv[:, :], t[:, 0:1], zv[:, :], ALU.mult, ALU.add).then_inc(rs_step, 1)
            dve.wait_ge(rs_step, 7)
            v.tensor_tensor(deg2[:, :], deg2[:, :], D[:, :], ALU.mult).then_inc(rs_step, 1)
            dve.wait_ge(rs_step, 8)
            v.tensor_scalar_add(deg2[:, :], deg2[:, :], 1.0).then_inc(rs_in, 1)
            split_L(4, 0)
            dve.wait_ge(rs_sqrt, 2)
            rsqrt_newton(w[:, :], deg2[:, :], rs_step, 8)
            v.tensor_tensor(c_col[:, :], D[:, :], w[:, :], ALU.mult).then_inc(rs_step, 1)
            dve.wait_ge(rs_step, 14)
            v.tensor_tensor(diag[:, :], c_col[:, :], deg[:, :], ALU.mult).then_inc(rs_step, 1)
            turn_vector(2, c_col[:, :])
            dve.wait_ge(rs_step, 15)
            dve.wait_ge(vec_in, 48)

            def add_terms(r):
                dve.wait_ge(gather_in, 16 * KEEP * (r + 1))
                nr = P if not isinstance(r, int) else rows(r)
                yr = y_out[0:nr, :, :].rearrange("p k f -> p (k f)")[:, bass.ds(r * F, F)]
                for j in range(KEEP):
                    if j:
                        dve.wait_ge(term_added, KEEP * r + j)
                    v.scalar_tensor_tensor(yr, gathered[0:nr, j, :], weight[0:nr, j:j + 1], yr,
                                           ALU.mult, ALU.add).then_inc(term_added, 1)

            def rank(r, slot, previous=True):
                dve.wait_ge(U_copied, r + 1)
                v.tensor_tensor(V[:, 0:N], prod_flat[:, bass.ds(slot * N, N)], vec_bc[:, :],
                                ALU.mult).then_inc(V_scaled, 1)
                dve.wait_ge(V_scaled, r + 1)
                v.scalar_tensor_tensor(V[:, bass.ds(r * P, P)], ident[:, :], diag[:, bass.ds(r, 1)],
                                       V[:, bass.ds(r * P, P)], ALU.mult, ALU.add).then_inc(V_ready, 1)
                dve.wait_ge(V_ready, r + 1)
                if previous:
                    add_terms(r - 1)
                v.max(top[:, :], V[:, 0:N]).then_inc(top_ready, 1)
                dve.wait_ge(top_ready, r + 1)
                if previous:
                    dve.wait_ge(term_added, KEEP * r)
                v.tensor_scalar(weight[:, :], top[:, 0:KEEP], c_col[:, bass.ds(r, 1)], None,
                                ALU.mult).then_inc(weight_ready, 1)
                v.max_index(index[:, :], top[:, :], V[:, 0:N]).then_inc(index_ready, 1)
                dve.wait_ge(weight_ready, r + 1)
                dve.wait_ge(index_ready, r + 1)

            rank(0, 0, previous=False)
            with dve.Fori(0, 3) as i:
                rank(2 * i + 1, (2 * i + 1) % XR)
                split_L(i + 5, (i + 1) % 2)
                rank(2 * i + 2, (2 * i + 2) % XR)
            with dve.Fori(7, FULL) as r:
                split_L(r + 1, (r + 1) % 2)
                rank(r, r % XR)

            r = FULL
            for n, (c0, c1) in enumerate(CH):
                dve.wait_ge(tail_chunk, n + 1)
                v.tensor_tensor(V[0:LAST, c0:c1], U[r % 2][0:LAST, c0:c1], vec_bc[0:LAST, c0:c1],
                                ALU.mult).then_inc(V_scaled, 1)
                if n == 0:
                    add_terms(r - 1)
                if n == 1:
                    dve.wait_ge(V_scaled, r + 2)
                    v.max(top2[0:LAST, 0:8], V[0:LAST, 0:c1]).then_inc(top_ready, 1)
            dve.wait_ge(V_scaled, r + 3)
            v.scalar_tensor_tensor(V[0:LAST, r * P:N], ident[0:LAST, 0:LAST], diag[0:LAST, r:r + 1],
                                   V[0:LAST, r * P:N], ALU.mult, ALU.add).then_inc(V_ready, 1)
            dve.wait_ge(V_ready, r + 1)
            v.max(top2[0:LAST, 8:16], V[0:LAST, CH[-1][0]:N]).then_inc(top_ready, 1)
            dve.wait_ge(top_ready, r + 2)
            v.max(top[0:LAST, :], top2[0:LAST, :]).then_inc(top_ready, 1)
            dve.wait_ge(top_ready, r + 3)
            v.max_index(index[0:LAST, :], top[0:LAST, :], V[0:LAST, 0:N]).then_inc(index_ready, 1)
            v.tensor_scalar(weight[0:LAST, :], top[0:LAST, 0:KEEP], c_col[0:LAST, r:r + 1], None,
                            ALU.mult).then_inc(weight_ready, 1)
            dve.wait_ge(weight_ready, r + 1)
            add_terms(r)

        @block.tensor
        def _(pe):
            mm = nc.tensor

            def transpose_bank(m_slot, c, bank):
                for k in BLK[c]:
                    ins = mm.transpose(T[0:rows(k), bank, (k % 4) * P:(k % 4 + 1) * P],
                                       row_stage[:, m_slot, k * P:k * P + rows(k)], ident[:, :])
                return ins

            def three_passes(p, k, c0, c1, cols):
                kr = rows(k)
                o = U[p][0:cols, c0:c1]
                hi = L_hi[0:kr, p, k * P:k * P + cols]
                lo = L_lo[0:kr, p, k * P:k * P + cols]
                mm.matmul(o, lo, A_hi[0:kr, k, c0:c1], start=(k == 0), stop=False)
                mm.matmul(o, hi, A_lo[0:kr, k, c0:c1], start=False, stop=False)
                return mm.matmul(o, hi, A_hi[0:kr, k, c0:c1], start=False, stop=(k == NT - 1))

            pe.wait_ge(ident_ready, 1)
            pe.wait_ge(stage_in[0], 16)
            transpose_bank(0, 0, 0)
            pe.wait_ge(small_in, 48)
            mm.transpose(WT_ps, W_sb[:, :], ident[0:F, 0:F])
            pe.wait_ge(h_ready, 1)
            for k in range(NT):
                ins = mm.transpose(hT_ps[:, k * P:(k + 1) * P], h[:, k, :], ident[:, :])
            ins.then_inc(hT_made, 1)
            pe.wait_ge(stage_in[1], 16)
            transpose_bank(1, 0, 1).then_inc(T_made, 1)
            pe.wait_ge(hT_copied, 2)
            for k in range(NT):
                ins = mm.matmul(g_ps[:, k, :], hT[:, k * P:(k + 1) * P], WT_sb[:, :], start=True, stop=True)
            ins.then_inc(g_made, 1)
            for k in range(NT):
                if k in (3, 7):
                    pe.wait_ge(T_used, k // 4 + 1)
                    transpose_bank(0, k // 4 + 1, 0)
                    transpose_bank(1, k // 4 + 1, 1).then_inc(T_made, 1)
                pe.wait_ge(lo_ready, k + 1)
                pe.wait_ge(hd_Llo, k + 1)
                if k == 0:
                    pe.wait_ge(g_copied, 1)
                for m in range(HEAD):
                    for c0, c1 in CH:
                        ins = three_passes(m, k, c0, c1, P)
                    if k == NT - 1:
                        ins.then_inc(U_done, 1)
            pe.wait_ge(stage_in[0], 32)
            for c in range(NC):
                pe.wait_ge(T_used, NC + max(c - 1, 0))
                transpose_bank(0, c, c % 2).then_inc(T_made, 1)

            def multiply(m, p):
                pe.wait_ge(Llo_ready, m - 1)
                pe.wait_ge(U_copied, m - 1)
                for n, (c0, c1) in enumerate(CH):
                    for k in range(NT):
                        ins = three_passes(p, k, c0, c1, P)
                    if n == len(CH) - 1:
                        ins.then_inc(U_done, 1)
                    for c in ((0, 1), (2,), ())[n]:
                        if c == 0:
                            pe.wait_ge(stage_in[1 - p], 8 * m + (16 if p == 0 else 24))
                        pe.wait_ge(T_used, 3 * m + (c - 1))
                        transpose_bank(1 - p, c, (1 - p + c) % 2).then_inc(T_made, 1)

            with pe.Fori(1, FULL // 2) as pair:
                multiply(2 * pair, 0)
                multiply(2 * pair + 1, 1)
            m = FULL
            pe.wait_ge(Llo_ready, m - 1)
            pe.wait_ge(U_copied, m - 1)
            for c0, c1 in CH:
                for k in range(NT):
                    ins = three_passes(m % 2, k, c0, c1, LAST)
                ins.then_inc(tail_chunk, 1)


_INS = ["x", "adj", "L0_gnn_theta", "L0_gnn_W", "L0_gnn_b"]


def kernel(**inputs):
    import numpy as _np
    import concourse.bacc as _bacc
    from concourse import mybir as _mybir
    from concourse.bass_utils import run_bass_kernel_spmd as _run

    nc = _bacc.Bacc("TRN2", target_bir_lowering=False, num_devices=1)
    arrays, args = {}, []
    for name in _INS:
        a = _np.ascontiguousarray(inputs[name])
        arrays[f"in_{name}_dram"] = a
        args.append(nc.dram_tensor(f"in_{name}_dram", a.shape, _mybir.dt.from_np(a.dtype), kind="ExternalInput").ap())
    out = nc.dram_tensor("out_dram", arrays["in_x_dram"].shape, _mybir.dt.float32, kind="ExternalOutput").ap()
    poly_graph_kernel(nc, *args, out)
    r = _run(nc, [arrays], core_ids=[0])
    return r.results[0]["out_dram"]
```

```python
from contextlib import ExitStack

import concourse.bass as bass
from concourse import mybir


def poly_graph_kernel(nc, x, adj, theta, W, b, out):
    f32, f32r, bf16, u32 = mybir.dt.float32, mybir.dt.float32r, mybir.dt.bfloat16, mybir.dt.uint32
    ALU, ACT, AX = mybir.AluOpType, mybir.ActivationFunctionType, mybir.AxisListType

    P = 128
    N, F = x.shape
    FULL = N // P
    NT = FULL + 1
    LAST = N - FULL * P
    NP = NT * P
    KEEP = 4
    EPS = 1e-5
    CH = [(c, min(c + 512, N)) for c in range(0, N, 512)]
    BLK = [range(c, min(c + 4, NT)) for c in range(0, NT, 4)]
    NC = len(BLK)
    RING = 3
    XR = 3
    HEAD = 2

    def rows(k):
        return P if k < FULL else LAST

    ctx = ExitStack()
    with ctx:
        def sb(name, shape, dt=f32):
            return ctx.enter_context(nc.sbuf_tensor(name, shape, dt))

        def sem(name):
            return ctx.enter_context(nc.semaphore(name))

        A_hi = sb("A_hi", [P, NT, N], f32r)
        A_lo = sb("A_lo", [P, NT, N], f32r)
        L_hi = sb("L_hi", [P, 2, NP], f32r)
        L_lo = sb("L_lo", [P, 2, NP], f32r)
        LT = sb("LT", [P, NP])
        row_stage = sb("row_stage", [P, 2, N])
        stream = sb("stream", [P, RING, N])
        prod = sb("prod", [P, XR, N])
        V = sb("V", [P, NP])
        vec_bc = sb("vec_bc", [P, N])
        y_out = sb("y_out", [P, NT, F])
        h = sb("h", [P, NT, F])
        ident = sb("ident", [P, P])
        t0_ident = sb("t0_ident", [P, P])
        gathered = sb("gathered", [P, KEEP, F])
        W_sb = sb("W_sb", [F, F])
        WT_sb = sb("WT_sb", [F, F])
        b_bc = sb("b_bc", [P, F])
        th = sb("th", [P, 2])
        t = sb("t", [P, 2])
        vec32 = sb("vec32", [P, 32])
        vec32T = sb("vec32T", [P, 32])
        deg = sb("deg", [P, NT])
        rdeg = sb("rdeg", [P, NT])
        s = sb("s", [P, NT])
        D = sb("D", [P, NT])
        yv = sb("yv", [P, NT])
        zv = sb("zv", [P, NT])
        deg2 = sb("deg2", [P, NT])
        w = sb("w", [P, NT])
        diag = sb("diag", [P, NT])
        c_col = sb("c_col", [P, NT])
        tmp = sb("tmp", [P, NT])
        mean = sb("mean", [P, NT])
        rstd = sb("rstd", [P, NT])
        top = sb("top", [P, 8])
        top2 = sb("top2", [P, 16])
        weight = sb("weight", [P, KEEP])
        index = sb("index", [P, 8], u32)
        xc = V[:, 0:NT * F].rearrange("p (k f) -> p k f", f=F)
        prod_flat = prod[:, :, :].rearrange("p a n -> p (a n)")
        hT = prod[0:F, 2, :]
        act_junk = prod[:, 2, :]
        head_LT = LT[:, 0:8 * P].rearrange("p (a m q) -> p a m q", m=2, q=P)

        U = [ctx.enter_context(nc.psum_tensor(f"U{i}", [P, 3 * 512], f32)) for i in range(2)]
        T = ctx.enter_context(nc.psum_tensor("T", [P, 2, 512], f32))
        hT_ps = U[1][0:F, 0:N]
        WT_ps = U[1][0:F, 3 * 512 - F:3 * 512]
        g_ps = U[1][:, 0:NT * F].rearrange("p (k f) -> p k f", f=F)

        g_dram = nc.dram_tensor("g_scratch", [N, F], f32).ap()
        vec_dram = nc.dram_tensor("vec_scratch", [NP], f32).ap()
        vec_cells = vec_dram.rearrange("(k b q) -> b k q", b=4, q=32)

        stage_in = [sem(f"stage_in{i}") for i in range(2)]
        stream_in = [sem(f"stream_in{i}") for i in range(RING)]
        x_in, theta_in, small_in = sem("x_in"), sem("theta_in"), sem("small_in")
        x_padded = sem("x_padded")
        ident_zero, ident_ready = sem("ident_zero"), sem("ident_ready")
        cleared = sem("cleared")
        th_exp, t_part, t_ready, t0i_ready = sem("th_exp"), sem("t_part"), sem("t_ready"), sem("t0i_ready")
        ln_sum, ln_mean, ln_step, ln_centered = sem("ln_sum"), sem("ln_mean"), sem("ln_step"), sem("ln_centered")
        ln_var, ln_sqrt_in, ln_sqrt, ln_newton, ln_rstd, h_ready = (
            sem("ln_var"), sem("ln_sqrt_in"), sem("ln_sqrt"), sem("ln_newton"), sem("ln_rstd"), sem("h_ready"))
        hT_made, hT_copied, g_made, g_copied, g_stored = (
            sem("hT_made"), sem("hT_copied"), sem("g_made"), sem("g_copied"), sem("g_stored"))
        xb_ready = sem("xb_ready")
        deg_ready, rdeg_ready, s_ready = sem("deg_ready"), sem("rdeg_ready"), sem("s_ready")
        hi_ready, lo_ready = sem("hi_ready"), sem("lo_ready")
        T_made, T_used = sem("T_made"), sem("T_used")
        hd_scaled, hd_diag, hd_Lhi, hd_Llo = sem("hd_scaled"), sem("hd_diag"), sem("hd_Lhi"), sem("hd_Llo")
        LT_scaled, LT_ready, Lhi_ready, Llo_ready = (
            sem("LT_scaled"), sem("LT_ready"), sem("Lhi_ready"), sem("Llo_ready"))
        U_done, U_copied, tail_chunk = sem("U_done"), sem("U_copied"), sem("tail_chunk")
        rs_in, rs_sqrt, rs_step = sem("rs_in"), sem("rs_sqrt"), sem("rs_step")
        vec_col, vec_turned, vec_stored, vec_in = sem("vec_col"), sem("vec_turned"), sem("vec_stored"), sem("vec_in")
        mv_done = sem("mv_done")
        V_scaled, V_ready, top_ready, index_ready, weight_ready = (
            sem("V_scaled"), sem("V_ready"), sem("top_ready"), sem("index_ready"), sem("weight_ready"))
        gather_begun, gather_in, term_added = sem("gather_begun"), sem("gather_in"), sem("term_added")
        out_stored = sem("out_stored")

        def T_count(m, c):
            return 3 * m + c - 1

        streamed = list(range(HEAD, NT)) + list(range(NT)) * 2
        MV1 = NT - HEAD
        MV2 = MV1 + NT

        block = ctx.enter_context(nc.Block())

        @block.sync
        def _(sp):
            def load_stage(m):
                sp.dma_start(row_stage[0:rows(m), m % 2, :],
                             adj[m * P:m * P + rows(m), :]).then_inc(stage_in[m % 2], 16)

            def load_stream(n):
                k = streamed[n]
                if n >= RING:
                    old = n - RING
                    if old < MV1:
                        sp.wait_ge(lo_ready, streamed[old] + 1)
                    else:
                        sp.wait_ge(mv_done, old - MV1 + 1)
                sp.dma_start(stream[0:rows(k), n % RING, :],
                             adj[k * P:k * P + rows(k), :]).then_inc(stream_in[n % RING], 16)

            def broadcast_vector(v):
                sp.wait_ge(vec_turned, v + 1)
                for q in range(4):
                    sp.dma_start(vec_cells[q], vec32T[32 * q:32 * q + NT, :]).then_inc(vec_stored, 16)
                sp.wait_ge(vec_stored, 64 * (v + 1))
                sp.dma_start(vec_bc[:, :], vec_dram[0:N].partition_broadcast(P)).then_inc(vec_in, 16)

            load_stage(0)
            load_stage(1)
            for n in range(MV1 + 1):
                load_stream(n)
            sp.wait_ge(lo_ready, HEAD)
            sp.wait_ge(T_made, NC + 1)
            load_stage(2)
            load_stage(3)
            broadcast_vector(0)
            for n in range(MV1 + 1, MV2 + RING):
                load_stream(n)
                if n == MV1 + 5:
                    sp.wait_ge(T_made, T_count(2, NC - 1))
                    load_stage(4)
                if n == MV1 + 8:
                    sp.wait_ge(T_made, T_count(3, NC - 1))
                    load_stage(5)
            broadcast_vector(1)
            for n in range(MV2 + RING, len(streamed)):
                load_stream(n)
            broadcast_vector(2)
            with sp.Fori(3, FULL // 2) as pair:
                for i in range(2):
                    sp.wait_ge(T_made, 6 * pair + (3 * i - 5))
                    sp.dma_start(row_stage[:, i, :],
                                 adj[bass.ds((2 * pair + i) * P, P), :]).then_inc(stage_in[i], 16)
            sp.wait_ge(T_made, T_count(FULL - 2, NC - 1))
            load_stage(FULL)
            sp.wait_ge(term_added, KEEP * FULL)
            sp.dma_start(out[0:FULL * P, :].rearrange("(k p) f -> p k f", p=P),
                         y_out[:, 0:FULL, :]).then_inc(out_stored, 16)
            sp.wait_ge(term_added, KEEP * NT)
            sp.dma_start(out[FULL * P:N, :], y_out[0:LAST, FULL, :]).then_inc(out_stored, 16)
            sp.wait_ge(out_stored, 32)

        @block.gpsimd
        def _(pool):
            nc.gpsimd.memset(y_out[:, FULL, :], 0.0).then_inc(x_padded, 1)
            nc.gpsimd.memset(ident[:, :], 0.0).then_inc(ident_zero, 1)
            pool.wait_ge(ident_zero, 1)
            nc.gpsimd.affine_select(out=ident[:, :], in_=ident[:, :], compare_op=ALU.not_equal, fill=1.0,
                                    base=0, pattern=[[-1, P]], channel_multiplier=1).then_inc(ident_ready, 1)
            pool.wait_ge(x_in, 32)
            mean_bc = mean[:, :].unsqueeze(2).to_broadcast([P, NT, F])
            rstd_bc = rstd[:, :].unsqueeze(2).to_broadcast([P, NT, F])
            pool.wait_ge(ln_mean, 1)
            nc.gpsimd.tensor_tensor(xc, y_out[:, :, :], mean_bc, ALU.subtract).then_inc(ln_step, 1)
            pool.wait_ge(ln_step, 1)
            nc.gpsimd.tensor_tensor(h[:, :, :], xc, xc, ALU.mult).then_inc(ln_centered, 1)
            nc.gpsimd.tensor_scalar(xc, xc, 0.0, None, ALU.max).then_inc(ln_step, 1)
            pool.wait_ge(small_in, 32)
            nc.gpsimd.tensor_tensor(y_out[:, :, :], y_out[:, :, :],
                                    b_bc[:, :].unsqueeze(1).to_broadcast([P, NT, F]), ALU.add).then_inc(xb_ready, 1)
            pool.wait_ge(ln_step, 2)
            pool.wait_ge(ln_rstd, 1)
            nc.gpsimd.tensor_tensor(h[:, :, :], xc, rstd_bc, ALU.mult).then_inc(h_ready, 1)
            pool.wait_ge(g_copied, 1)
            pool.dma_start(g_dram[0:FULL * P, :].rearrange("(k p) f -> p k f", p=P),
                           h[:, 0:FULL, :]).then_inc(g_stored, 16)
            pool.dma_start(g_dram[FULL * P:N, :], h[0:LAST, FULL, :]).then_inc(g_stored, 16)
            pool.wait_ge(g_stored, 32)
            with pool.Fori(0, FULL) as r:
                pool.wait_ge(index_ready, r + 1)
                pool.sem_inc(gather_begun, 1)
                for j in range(KEEP):
                    nc.gpsimd.indirect_dma_start(
                        gathered[:, j, :], None, g_dram[:, :],
                        bass.IndirectOffsetOnAxis(ap=index[:, j:j + 1], axis=0)).then_inc(gather_in, 16)
            pool.wait_ge(index_ready, NT)
            for j in range(KEEP):
                nc.gpsimd.indirect_dma_start(
                    gathered[0:LAST, j, :], None, g_dram[:, :],
                    bass.IndirectOffsetOnAxis(ap=index[0:LAST, j:j + 1], axis=0)).then_inc(gather_in, 16)

        @block.scalar
        def _(act):
            act.dma_start(th[:, :], theta.partition_broadcast(P)).then_inc(theta_in, 16)
            act.wait_ge(theta_in, 16)
            nc.scalar.activation(t[:, :], th[:, :], ACT.Exp, scale=-1.0).then_inc(th_exp, 1)

            def row_sum(k):
                if k < HEAD:
                    act.wait_ge(stage_in[k], 16)
                    src = row_stage[:, k, :]
                else:
                    n = k - HEAD
                    act.wait_ge(stream_in[n % RING], 16 * (n // RING + 1))
                    src = stream[0:rows(k), n % RING, :]
                if k:
                    act.wait_ge(deg_ready, k)
                nc.scalar.activation(act_junk[0:rows(k), :], src, ACT.Copy,
                                     accum_out=deg[0:rows(k), k:k + 1]).then_inc(deg_ready, 1)

            def head_scale(k, m0, m1, count):
                kr = rows(k)
                nc.scalar.activation(head_LT[0:kr, k % 4, m0:m1, :], T[0:kr, m0:m1, (k % 4) * P:(k % 4 + 1) * P],
                                     ACT.Copy, scale=s[0:kr, k:k + 1]).then_inc(hd_scaled, 1)
                act.wait_ge(hd_scaled, count)

            def head_high(k, m0, m1):
                kr = rows(k)
                nc.scalar.activation(L_hi[0:kr, m0:m1, k * P:(k + 1) * P], head_LT[0:kr, k % 4, m0:m1, :],
                                     ACT.Copy).then_inc(hd_Lhi, 1)

            act.wait_ge(cleared, 1)
            row_sum(0)
            act.wait_ge(T_made, 1)
            act.wait_ge(s_ready, 1)
            head_scale(0, 0, 1, 1)
            act.wait_ge(hd_diag, 1)
            head_high(0, 0, 1)
            act.wait_ge(T_made, 2)
            head_scale(0, 1, 2, 2)
            head_high(0, 1, 2)
            row_sum(1)
            act.wait_ge(x_padded, 1)
            act.dma_start(y_out[:, 0:FULL, :], x[0:FULL * P, :].rearrange("(k p) f -> p k f", p=P)).then_inc(x_in, 16)
            act.dma_start(y_out[0:LAST, FULL, :], x[FULL * P:N, :]).then_inc(x_in, 16)
            act.dma_start(b_bc[:, :], b.partition_broadcast(P)).then_inc(small_in, 16)
            act.dma_start(W_sb[:, :], W).then_inc(small_in, 16)
            for k in range(1, NT):
                if k % 4 == 0:
                    act.wait_ge(T_made, k // 4 + 2)
                if k + 1 < NT:
                    row_sum(k + 1)
                act.wait_ge(s_ready, k + 1)
                if k >= 4:
                    act.wait_ge(hd_Llo, k - 2)
                head_scale(k, 0, 2, k + 2)
                if k < HEAD:
                    act.wait_ge(hd_diag, k + 1)
                if k % 4 == 3 or k == NT - 1:
                    act.sem_inc(T_used, 1)
                head_high(k, 0, 2)
                if k == 6:
                    act.wait_ge(ln_sqrt_in, 1)
                    nc.scalar.activation(rstd[:, :], mean[:, :], ACT.Sqrt).then_inc(ln_sqrt, 1)
                if k == NT - 2:
                    act.wait_ge(rs_in, 1)
                    nc.scalar.activation(D[:, :], deg[:, :], ACT.Sqrt).then_inc(rs_sqrt, 1)

            def scale_bank(c, bank):
                for k in BLK[c]:
                    ins = nc.scalar.activation(LT[0:rows(k), k * P:(k + 1) * P],
                                               T[0:rows(k), bank, (k % 4) * P:(k % 4 + 1) * P],
                                               ACT.Copy, scale=s[0:rows(k), k:k + 1])
                return ins

            def scale_tile(m, bank0):
                act.wait_ge(Llo_ready, m - 3 + NC)
                for c in range(NC):
                    act.wait_ge(T_made, 3 * m + (c - 1))
                    scale_bank(c, (bank0 + c) % 2).then_inc(T_used, 1)

            def high_tile(m, p):
                act.wait_ge(LT_ready, m - 1)
                act.wait_ge(U_done, m - 1)
                nc.scalar.activation(L_hi[:, p, :], LT[:, :], ACT.Copy).then_inc(Lhi_ready, 1)

            def copy_product(m, p, slot):
                act.wait_ge(U_done, m + 1)
                nc.scalar.activation(prod_flat[:, bass.ds(slot * N, N)],
                                     U[p][:, 0:N], ACT.Copy).then_inc(U_copied, 1)

            for c in range(NC):
                act.wait_ge(hd_Llo, (10, 12, 12)[c])
                act.wait_ge(T_made, T_count(2, c))
                scale_bank(c, c % 2).then_inc(T_used, 1)
                act.wait_ge(T_used, NC + c + 1)
                if c == 0:
                    act.wait_ge(LT_ready, 1)
                if c == NC - 1:
                    act.wait_ge(U_done, 1)
                cols = slice(BLK[c][0] * P, (BLK[c][-1] + 1) * P)
                nc.scalar.activation(L_hi[:, 0, cols], LT[:, cols], ACT.Copy).then_inc(Lhi_ready, 1)
                if c == 0:
                    copy_product(0, 0, 0)
            copy_product(1, 1, 1)
            scale_tile(3, 1)
            act.wait_ge(hT_made, 1)
            nc.scalar.activation(hT, hT_ps, ACT.Copy).then_inc(hT_copied, 1)
            nc.scalar.activation(WT_sb[:, :], WT_ps, ACT.Copy).then_inc(hT_copied, 1)
            high_tile(3, 1)
            act.wait_ge(g_made, 1)
            nc.scalar.activation(h[:, :, :], g_ps, ACT.Copy).then_inc(g_copied, 1)
            scale_tile(4, 0)
            high_tile(4, 0)
            copy_product(2, 0, 2)
            act.wait_ge(rs_in, 2)
            nc.scalar.activation(w[:, :], deg2[:, :], ACT.Sqrt).then_inc(rs_sqrt, 1)
            with act.Fori(2, FULL // 2) as pair:
                for i in range(2):
                    m = 2 * pair
                    scale_tile(m + (i + 1), (i + 1) % 2)
                    high_tile(m + (i + 1), (i + 1) % 2)
                    act.wait_ge(V_scaled, m + (i - 3))
                    copy_product(m + (i - 1), (i + 1) % 2, (m + (i - 1)) % XR)
            act.wait_ge(V_scaled, FULL - 3)
            copy_product(FULL - 1, 1, (FULL - 1) % XR)

        @block.vector
        def _(dve):
            v = nc.vector

            def rsqrt_newton(dst, src, step_sem, base):
                v.reciprocal(dst, dst).then_inc(step_sem, 1)
                dve.wait_ge(step_sem, base + 1)
                v.tensor_tensor(tmp[:, :], dst, dst, ALU.mult).then_inc(step_sem, 1)
                dve.wait_ge(step_sem, base + 2)
                v.tensor_tensor(tmp[:, :], tmp[:, :], src, ALU.mult).then_inc(step_sem, 1)
                dve.wait_ge(step_sem, base + 3)
                v.tensor_scalar(tmp[:, :], tmp[:, :], -0.5, 1.5, ALU.mult, ALU.add).then_inc(step_sem, 1)
                dve.wait_ge(step_sem, base + 4)
                v.tensor_tensor(dst, dst, tmp[:, :], ALU.mult).then_inc(step_sem, 1)
                dve.wait_ge(step_sem, base + 5)

            v.memset(vec32[:, :], 0.0)
            v.memset(yv[:, :], 0.0)
            v.memset(zv[:, :], 0.0)
            v.memset(LT[:, FULL * P:NP], 0.0)
            v.memset(deg[:, :], 1.0).then_inc(cleared, 1)

            dve.wait_ge(th_exp, 1)
            v.tensor_scalar_add(t[:, :], t[:, :], 1.0).then_inc(t_part, 1)
            dve.wait_ge(t_part, 1)
            v.reciprocal(t[:, :], t[:, :]).then_inc(t_ready, 1)
            dve.wait_ge(t_ready, 1)
            dve.wait_ge(ident_ready, 1)
            v.tensor_scalar(t0_ident[:, :], ident[:, :], t[:, 0:1], None, ALU.mult).then_inc(t0i_ready, 1)

            def source(k):
                return row_stage[:, k, :] if k < HEAD else stream[0:rows(k), (k - HEAD) % RING, :]

            def high(k):
                if k < HEAD:
                    dve.wait_ge(stage_in[k], 16)
                else:
                    dve.wait_ge(stream_in[(k - HEAD) % RING], 16 * ((k - HEAD) // RING + 1))
                v.tensor_copy(A_hi[0:rows(k), k, :], source(k)).then_inc(hi_ready, 1)

            def low(k):
                dve.wait_ge(hi_ready, k + 1)
                v.tensor_tensor(A_lo[0:rows(k), k, :], source(k), A_hi[0:rows(k), k, :].bitcast(f32),
                                ALU.subtract).then_inc(lo_ready, 1)

            def scale_of(k):
                dve.wait_ge(deg_ready, k + 1)
                v.reciprocal(rdeg[:, k:k + 1], deg[:, k:k + 1]).then_inc(rdeg_ready, 1)
                dve.wait_ge(rdeg_ready, k + 1)
                v.tensor_scalar(s[:, k:k + 1], rdeg[:, k:k + 1], t[:, 1:2], None, ALU.mult).then_inc(s_ready, 1)

            def head_diagonal(k, count):
                dve.wait_ge(hd_scaled, count)
                v.tensor_tensor(head_LT[:, k, k, :], head_LT[:, k, k, :], t0_ident[:, :], ALU.add).then_inc(hd_diag, 1)

            def head_low(k, m0, m1, count):
                dve.wait_ge(hd_Lhi, count)
                kr = rows(k)
                v.tensor_tensor(L_lo[0:kr, m0:m1, k * P:(k + 1) * P], head_LT[0:kr, k % 4, m0:m1, :],
                                L_hi[0:kr, m0:m1, k * P:(k + 1) * P].bitcast(f32), ALU.subtract).then_inc(hd_Llo, 1)

            def turn_vector(n, col):
                v.tensor_copy(vec32[:, 0:NT], col).then_inc(vec_col, 1)
                dve.wait_ge(vec_col, n + 1)
                if n >= 1:
                    dve.wait_ge(vec_stored, 64 * n)
                v.transpose(vec32T[:, :], vec32[:, :]).then_inc(vec_turned, 1)

            dve.wait_ge(t0i_ready, 1)
            high(0)
            scale_of(0)
            low(0)
            head_diagonal(0, 1)
            head_low(0, 0, 1, 1)
            high(1)
            head_low(0, 1, 2, 2)
            scale_of(1)
            low(1)
            head_diagonal(1, 3)
            for k in range(1, NT):
                if k + 1 < NT:
                    high(k + 1)
                    scale_of(k + 1)
                head_low(k, 0, 2, k + 2)
                if k + 1 < NT:
                    low(k + 1)
                if k == 4:
                    dve.wait_ge(x_in, 32)
                    v.reduce_sum(mean[:, :], y_out[:, :, :], AX.X).then_inc(ln_sum, 1)
                    dve.wait_ge(ln_sum, 1)
                    v.tensor_scalar(mean[:, :], mean[:, :], 1.0 / F, None, ALU.mult).then_inc(ln_mean, 1)
                if k == 6:
                    dve.wait_ge(ln_centered, 1)
                    v.reduce_sum(mean[:, :], h[:, :, :], AX.X).then_inc(ln_var, 1)
                    dve.wait_ge(ln_var, 1)
                    v.tensor_scalar(mean[:, :], mean[:, :], 1.0 / F, EPS, ALU.mult, ALU.add).then_inc(ln_sqrt_in, 1)
                if k == 7:
                    dve.wait_ge(ln_sqrt_in, 1)
                    dve.wait_ge(ln_sqrt, 1)
                    rsqrt_newton(rstd[:, :], mean[:, :], ln_newton, 0)
                    dve.sem_inc(ln_rstd, 1)
                if k == NT - 2:
                    v.tensor_scalar(deg[:, :], deg[:, :], 1.0, None, ALU.mult).then_inc(rs_in, 1)
                    dve.wait_ge(rs_sqrt, 1)
                    rsqrt_newton(D[:, :], deg[:, :], rs_step, 0)
                    turn_vector(0, D[:, :])

            def add_diagonal(m):
                dve.wait_ge(T_used, 3 * m)
                v.tensor_tensor(LT[:, bass.ds(m * P, P)], LT[:, bass.ds(m * P, P)], t0_ident[:, :],
                                ALU.add).then_inc(LT_ready, 1)

            def low_L(m, p):
                dve.wait_ge(Lhi_ready, m - 2 + NC)
                v.tensor_tensor(L_lo_flat[:, bass.ds(p * NP, NP)], LT[:, :],
                                L_hi_flat[:, bass.ds(p * NP, NP)].bitcast(f32),
                                ALU.subtract).then_inc(Llo_ready, 1)

            def low_L2(c):
                cols = slice(BLK[c][0] * P, (BLK[c][-1] + 1) * P)
                dve.wait_ge(Lhi_ready, c + 1)
                v.tensor_tensor(L_lo[:, 0, cols], LT[:, cols], L_hi[:, 0, cols].bitcast(f32),
                                ALU.subtract).then_inc(Llo_ready, 1)

            L_lo_flat = L_lo[:, :, :].rearrange("p a n -> p (a n)")
            L_hi_flat = L_hi[:, :, :].rearrange("p a n -> p (a n)")

            def times_vector(n, dst, k0, k1):
                dve.wait_ge(vec_in, 16 * (n + 1))
                for k in range(k0, k1):
                    i = (MV1, MV2)[n] + k
                    dve.wait_ge(stream_in[i % RING], 16 * (i // RING + 1))
                    if NT * n + k:
                        dve.wait_ge(mv_done, NT * n + k)
                    v.tensor_tensor_reduce(out=V[0:rows(k), 0:N], in0=stream[0:rows(k), i % RING, :],
                                           in1=vec_bc[0:rows(k), :], scale=1.0, scalar=0.0,
                                           op0=ALU.mult, op1=ALU.add,
                                           accum_out=dst[0:rows(k), k:k + 1]).then_inc(mv_done, 1)

            dve.wait_ge(T_used, NC + 1)
            v.tensor_tensor(LT[:, 2 * P:3 * P], LT[:, 2 * P:3 * P], t0_ident[:, :], ALU.add).then_inc(LT_ready, 1)
            low_L2(0)
            low_L2(1)
            dve.wait_ge(h_ready, 1)
            times_vector(0, yv, 0, 1)
            low_L2(2)
            times_vector(0, yv, 1, 5)
            add_diagonal(3)
            times_vector(0, yv, 5, 8)
            low_L(3, 1)
            times_vector(0, yv, 8, NT)
            dve.wait_ge(mv_done, NT)
            v.tensor_tensor(tmp[:, :], s[:, :], yv[:, :], ALU.mult).then_inc(rs_step, 1)
            dve.wait_ge(rs_step, 6)
            turn_vector(1, tmp[:, :])
            times_vector(1, zv, 0, 5)
            add_diagonal(4)
            times_vector(1, zv, 5, 6)
            low_L(4, 0)
            times_vector(1, zv, 6, NT)
            dve.wait_ge(mv_done, 2 * NT)
            v.scalar_tensor_tensor(deg2[:, :], yv[:, :], t[:, 0:1], zv[:, :], ALU.mult, ALU.add).then_inc(rs_step, 1)
            dve.wait_ge(rs_step, 7)
            v.tensor_tensor(deg2[:, :], deg2[:, :], D[:, :], ALU.mult).then_inc(rs_step, 1)
            dve.wait_ge(rs_step, 8)
            v.tensor_scalar_add(deg2[:, :], deg2[:, :], 1.0).then_inc(rs_in, 1)
            dve.wait_ge(rs_sqrt, 2)
            rsqrt_newton(w[:, :], deg2[:, :], rs_step, 8)
            v.tensor_tensor(c_col[:, :], D[:, :], w[:, :], ALU.mult).then_inc(rs_step, 1)
            dve.wait_ge(rs_step, 14)
            v.tensor_tensor(diag[:, :], c_col[:, :], deg[:, :], ALU.mult).then_inc(rs_step, 1)
            turn_vector(2, c_col[:, :])
            dve.wait_ge(rs_step, 15)
            dve.wait_ge(vec_in, 48)

            def add_terms(r):
                dve.wait_ge(gather_in, 16 * KEEP * (r + 1))
                nr = P if not isinstance(r, int) else rows(r)
                yr = y_out[0:nr, :, :].rearrange("p k f -> p (k f)")[:, bass.ds(r * F, F)]
                for j in range(KEEP):
                    if j:
                        dve.wait_ge(term_added, KEEP * r + j)
                    v.scalar_tensor_tensor(yr, gathered[0:nr, j, :], weight[0:nr, j:j + 1], yr,
                                           ALU.mult, ALU.add).then_inc(term_added, 1)

            def rank(r, slot, previous=True):
                dve.wait_ge(U_copied, r + 1)
                v.tensor_tensor(V[:, 0:N], prod_flat[:, bass.ds(slot * N, N)], vec_bc[:, :],
                                ALU.mult).then_inc(V_scaled, 1)
                dve.wait_ge(V_scaled, r + 1)
                v.scalar_tensor_tensor(V[:, bass.ds(r * P, P)], ident[:, :], diag[:, bass.ds(r, 1)],
                                       V[:, bass.ds(r * P, P)], ALU.mult, ALU.add).then_inc(V_ready, 1)
                dve.wait_ge(V_ready, r + 1)
                if previous:
                    add_terms(r - 1)
                v.max(top[:, :], V[:, 0:N]).then_inc(top_ready, 1)
                dve.wait_ge(top_ready, r + 1)
                if previous:
                    dve.wait_ge(term_added, KEEP * r)
                v.tensor_scalar(weight[:, :], top[:, 0:KEEP], c_col[:, bass.ds(r, 1)], None,
                                ALU.mult).then_inc(weight_ready, 1)
                v.max_index(index[:, :], top[:, :], V[:, 0:N]).then_inc(index_ready, 1)
                dve.wait_ge(weight_ready, r + 1)
                dve.wait_ge(index_ready, r + 1)

            rank(0, 0, previous=False)
            with dve.Fori(0, 2) as i:
                add_diagonal(i + 5)
                rank(2 * i + 1, (2 * i + 1) % XR)
                low_L(i + 5, (i + 1) % 2)
                rank(2 * i + 2, (2 * i + 2) % XR)
            with dve.Fori(5, FULL - 1) as r:
                add_diagonal(r + 2)
                low_L(r + 2, r % 2)
                rank(r, r % XR)
            rank(FULL - 1, (FULL - 1) % XR)

            r = FULL
            for n, (c0, c1) in enumerate(CH):
                dve.wait_ge(tail_chunk, n + 1)
                v.tensor_tensor(V[0:LAST, c0:c1], U[r % 2][0:LAST, c0:c1], vec_bc[0:LAST, c0:c1],
                                ALU.mult).then_inc(V_scaled, 1)
                if n == 0:
                    add_terms(r - 1)
                if n == 1:
                    dve.wait_ge(V_scaled, r + 2)
                    v.max(top2[0:LAST, 0:8], V[0:LAST, 0:c1]).then_inc(top_ready, 1)
            dve.wait_ge(V_scaled, r + 3)
            v.scalar_tensor_tensor(V[0:LAST, r * P:N], ident[0:LAST, 0:LAST], diag[0:LAST, r:r + 1],
                                   V[0:LAST, r * P:N], ALU.mult, ALU.add).then_inc(V_ready, 1)
            dve.wait_ge(V_ready, r + 1)
            v.max(top2[0:LAST, 8:16], V[0:LAST, CH[-1][0]:N]).then_inc(top_ready, 1)
            dve.wait_ge(top_ready, r + 2)
            v.max(top[0:LAST, :], top2[0:LAST, :]).then_inc(top_ready, 1)
            dve.wait_ge(top_ready, r + 3)
            v.max_index(index[0:LAST, :], top[0:LAST, :], V[0:LAST, 0:N]).then_inc(index_ready, 1)
            v.tensor_scalar(weight[0:LAST, :], top[0:LAST, 0:KEEP], c_col[0:LAST, r:r + 1], None,
                            ALU.mult).then_inc(weight_ready, 1)
            dve.wait_ge(weight_ready, r + 1)
            add_terms(r)

        @block.tensor
        def _(pe):
            mm = nc.tensor

            def transpose_bank(m_slot, c, bank):
                for k in BLK[c]:
                    ins = mm.transpose(T[0:rows(k), bank, (k % 4) * P:(k % 4 + 1) * P],
                                       row_stage[:, m_slot, k * P:k * P + rows(k)], ident[:, :])
                return ins

            def three_passes(p, k, c0, c1, cols):
                kr = rows(k)
                o = U[p][0:cols, c0:c1]
                hi = L_hi[0:kr, p, k * P:k * P + cols]
                lo = L_lo[0:kr, p, k * P:k * P + cols]
                mm.matmul(o, lo, A_hi[0:kr, k, c0:c1], start=(k == 0), stop=False)
                mm.matmul(o, hi, A_lo[0:kr, k, c0:c1], start=False, stop=False)
                return mm.matmul(o, hi, A_hi[0:kr, k, c0:c1], start=False, stop=(k == NT - 1))

            pe.wait_ge(ident_ready, 1)
            pe.wait_ge(stage_in[0], 16)
            transpose_bank(0, 0, 0).then_inc(T_made, 1)
            pe.wait_ge(stage_in[1], 16)
            transpose_bank(1, 0, 1).then_inc(T_made, 1)
            for k in range(NT):
                if k in (3, 7):
                    pe.wait_ge(T_used, k // 4 + 1)
                    transpose_bank(0, k // 4 + 1, 0)
                    transpose_bank(1, k // 4 + 1, 1).then_inc(T_made, 1)
                if k == NT - 1:
                    pe.wait_ge(stage_in[0], 32)
                    pe.wait_ge(T_used, NC)
                    transpose_bank(0, 0, 0).then_inc(T_made, 1)
                    transpose_bank(0, 1, 1).then_inc(T_made, 1)
                pe.wait_ge(lo_ready, k + 1)
                for m in range(HEAD):
                    if k == 0:
                        pe.wait_ge(hd_Llo, m + 1)
                    elif m == 0:
                        pe.wait_ge(hd_Llo, k + 2)
                    for c0, c1 in CH:
                        ins = three_passes(m, k, c0, c1, P)
                    if k == NT - 1:
                        ins.then_inc(U_done, 1)
            pe.wait_ge(T_used, NC + 1)
            transpose_bank(0, 2, 0).then_inc(T_made, 1)

            def transpose_h():
                pe.wait_ge(U_copied, 2)
                pe.wait_ge(h_ready, 1)
                for k in range(NT):
                    mm.transpose(hT_ps[:, k * P:k * P + rows(k)], h[0:rows(k), k, :], ident[0:rows(k), 0:rows(k)])
                pe.wait_ge(small_in, 32)
                mm.transpose(WT_ps, W_sb[:, :], ident[0:F, 0:F]).then_inc(hT_made, 1)

            def multiply_h():
                pe.wait_ge(hT_copied, 2)
                for k in range(NT):
                    ins = mm.matmul(g_ps[0:rows(k), k, :], hT[:, k * P:k * P + rows(k)], WT_sb[:, :],
                                    start=True, stop=True)
                ins.then_inc(g_made, 1)

            def multiply(m, p, first=False):
                if not first:
                    pe.wait_ge(Llo_ready, m - 2 + NC)
                pe.wait_ge(U_copied, m - 1)
                for n, (c0, c1) in enumerate(CH):
                    for k in range(NT):
                        if first and n == 0 and k % 4 == 0:
                            pe.wait_ge(Llo_ready, k // 4 + 1)
                        ins = three_passes(p, k, c0, c1, P)
                        for c in {(0, 0): (0, 1), (0, 6): (2,)}.get((n, k), ()):
                            if c == 0:
                                pe.wait_ge(stage_in[1 - p], 8 * m + (16 if p == 0 else 24))
                            pe.wait_ge(T_used, 3 * m + (c - 1))
                            transpose_bank(1 - p, c, (1 - p + c) % 2).then_inc(T_made, 1)
                    if first and n == 0:
                        transpose_h()
                    if first and n == 1:
                        multiply_h()
                    if n == len(CH) - 1:
                        ins.then_inc(U_done, 1)

            multiply(2, 0, first=True)
            pe.wait_ge(g_copied, 1)
            multiply(3, 1)
            with pe.Fori(2, FULL // 2) as pair:
                multiply(2 * pair, 0)
                multiply(2 * pair + 1, 1)
            m = FULL
            pe.wait_ge(Llo_ready, m - 2 + NC)
            pe.wait_ge(U_copied, m - 1)
            for c0, c1 in CH:
                for k in range(NT):
                    ins = three_passes(m % 2, k, c0, c1, LAST)
                ins.then_inc(tail_chunk, 1)


_INS = ["x", "adj", "L0_gnn_theta", "L0_gnn_W", "L0_gnn_b"]


def kernel(**inputs):
    import numpy as _np
    import concourse.bacc as _bacc
    from concourse import mybir as _mybir
    from concourse.bass_utils import run_bass_kernel_spmd as _run

    nc = _bacc.Bacc("TRN2", target_bir_lowering=False, num_devices=1)
    arrays, args = {}, []
    for name in _INS:
        a = _np.ascontiguousarray(inputs[name])
        arrays[f"in_{name}_dram"] = a
        args.append(nc.dram_tensor(f"in_{name}_dram", a.shape, _mybir.dt.from_np(a.dtype), kind="ExternalInput").ap())
    out = nc.dram_tensor("out_dram", arrays["in_x_dram"].shape, _mybir.dt.float32, kind="ExternalOutput").ap()
    poly_graph_kernel(nc, *args, out)
    r = _run(nc, [arrays], core_ids=[0])
    return r.results[0]["out_dram"]
```

```python
from contextlib import ExitStack

import concourse.bass as bass
from concourse import mybir


def poly_graph_kernel(nc, x, adj, theta, W, b, out):
    f32, f32r, u32 = mybir.dt.float32, mybir.dt.float32r, mybir.dt.uint32
    ALU, ACT, AX = mybir.AluOpType, mybir.ActivationFunctionType, mybir.AxisListType

    P = 128
    N, F = x.shape
    FULL = N // P
    NT = FULL + 1
    LAST = N - FULL * P
    NB = NT + 1
    MIX = FULL
    CUT = P - LAST
    NP = NB * P
    NS = N + 2 * LAST
    G = 32
    GROUPS = P // G
    SPAN = FULL * G
    MAIN = FULL * P
    KEEP = 4
    EPS = 1e-5
    CH = [(c, min(c + 512, N)) for c in range(0, N, 512)]
    BLK = [range(c, min(c + 4, NB)) for c in range(0, NB, 4)]
    NC = len(BLK)
    PIECES = [range(0, 1), range(1, 4)] + BLK[1:]
    RING = 3
    XR = 6
    LATE = 7
    HEAD = 2

    def rows(k):
        return P if k < FULL else LAST

    def lanes(k):
        return P if k <= MIX else NS - NT * P

    ctx = ExitStack()
    with ctx:
        def sb(name, shape, dt=f32):
            return ctx.enter_context(nc.sbuf_tensor(name, shape, dt))

        def sem(name):
            return ctx.enter_context(nc.semaphore(name))

        A_hi = sb("A_hi", [P, NT, N], f32r)
        A_lo = sb("A_lo", [P, NT, N], f32r)
        L_hi = sb("L_hi", [P, 2, NP], f32r)
        L_lo = sb("L_lo", [P, 2, MIX * P], f32r)
        LT = sb("LT", [P, NP])
        row_stage = sb("row_stage", [P, 2, NS])
        prod = sb("prod", [P, XR, N])
        stream = [prod[:, i, :] for i in (4, 3, 5)]
        V = sb("V", [P, N])
        vec_bc = sb("vec_bc", [P, MAIN + 3 * G])
        y_out = sb("y_out", [P, NT, F])
        h = sb("h", [P, NT, F])
        ident = sb("ident", [P, P])
        t0_ident = sb("t0_ident", [P, P])
        low_of_L = sb("low_of_L", [P, 2])
        sign_of_A = sb("sign_of_A", [P, 1])
        low_of_A = sb("low_of_A", [P, 1])
        gathered_0 = sb("gathered_0", [P, KEEP, F])
        b_bc = sb("b_bc", [P, F])
        th = sb("th", [P, 2])
        t = sb("t", [P, 2])
        vec32 = sb("vec32", [P, 32])
        vec32T = sb("vec32T", [P, 32])
        deg = sb("deg", [P, NB])
        rdeg = sb("rdeg", [P, NB])
        s = sb("s", [P, NB])
        D = sb("D", [P, NT])
        yv = sb("yv", [P, NT])
        zv = sb("zv", [P, NT])
        deg2 = sb("deg2", [P, NT])
        w = sb("w", [P, NT])
        diag = sb("diag", [P, NT])
        c_col = sb("c_col", [P, NT])
        tmp = sb("tmp", [P, NT])
        mean = sb("mean", [P, NT])
        rstd = sb("rstd", [P, NT])
        top = sb("top", [P, 8])
        top2 = sb("top2", [P, 16])
        weight = sb("weight", [P, 2, KEEP])
        index = sb("index", [P, 2, 8], u32)
        prod_flat = prod[:, :, :].rearrange("p a n -> p (a n)")
        hT = prod[0:F, 2, :]
        W_sb, WT_sb = gathered_0[0:F, 0, :], gathered_0[0:F, 1, :]
        act_junk = prod[:, 2, :]
        xc = prod[:, 2, 0:NT * F].rearrange("p (k f) -> p k f", f=F)
        LT2 = V[:, 0:MAIN]
        in_blocks = [V[:, 0:MAIN], vec_bc[:, 0:MAIN]]
        head_LT = LT[:, 0:8 * P].rearrange("p (a m q) -> p a m q", m=2, q=P)

        gathered = [gathered_0, h[:, 4:4 + KEEP, :]]
        mix_ident = h[:, 0:2 * P // F, :].rearrange("p k f -> p (k f)")

        U = [ctx.enter_context(nc.psum_tensor(f"U{i}", [P, 3 * 512], f32)) for i in range(2)]
        T = ctx.enter_context(nc.psum_tensor("T", [P, 2, 512], f32))
        hT_ps = U[1][0:F, 0:N]
        WT_ps = U[1][0:F, 3 * 512 - F:3 * 512]
        g_ps = U[1][:, 0:NT * F].rearrange("p (k f) -> p k f", f=F)

        g_dram = nc.dram_tensor("g_scratch", [N, F], f32).ap()
        vec_dram = nc.dram_tensor("vec_scratch", [NT * P], f32).ap()
        vec_cells = vec_dram.rearrange("(b k q) -> b k q", b=GROUPS, q=G)

        stage_in = [sem(f"stage_in{i}") for i in range(2)]
        late_stage_in = sem("late_stage_in")
        head_blocks = sem("head_blocks")
        head_again, again_ready, LT_turned = sem("head_again"), sem("again_ready"), sem("LT_turned")
        stream_in = [sem(f"stream_in{i}") for i in range(RING + 2)]
        x_in, theta_in, small_in = sem("x_in"), sem("theta_in"), sem("small_in")
        x_padded = sem("x_padded")
        ident_zero, ident_ready = sem("ident_zero"), sem("ident_ready")
        mix_step, masks_ready, mix_ident_ready = sem("mix_step"), sem("masks_ready"), sem("mix_ident_ready")
        cleared = sem("cleared")
        th_exp, t_part, t_ready, t0i_ready = sem("th_exp"), sem("t_part"), sem("t_ready"), sem("t0i_ready")
        ln_sum, ln_mean, ln_step, ln_centered = sem("ln_sum"), sem("ln_mean"), sem("ln_step"), sem("ln_centered")
        ln_var, ln_sqrt_in, ln_sqrt, ln_newton, ln_rstd, h_ready = (
            sem("ln_var"), sem("ln_sqrt_in"), sem("ln_sqrt"), sem("ln_newton"), sem("ln_rstd"), sem("h_ready"))
        hT_made, hT_copied, g_made, g_copied, g_stored = (
            sem("hT_made"), sem("hT_copied"), sem("g_made"), sem("g_copied"), sem("g_stored"))
        xb_ready = sem("xb_ready")
        deg_ready, rdeg_ready, s_ready = sem("deg_ready"), sem("rdeg_ready"), sem("s_ready")
        hi_ready, lo_ready, tile1_low = sem("hi_ready"), sem("lo_ready"), sem("tile1_low")
        T_made, T_used = sem("T_made"), sem("T_used")
        hd_scaled, hd_diag, hd_Lhi, hd_Llo = sem("hd_scaled"), sem("hd_diag"), sem("hd_Lhi"), sem("hd_Llo")
        LT2_scaled, LT_scaled, LT_ready, Lhi_ready, Llo_ready = (
            sem("LT2_scaled"), sem("LT_scaled"), sem("LT_ready"), sem("Lhi_ready"), sem("Llo_ready"))
        U_done, U_copied, tail_chunk = sem("U_done"), sem("U_copied"), sem("tail_chunk")
        rs_in, rs_sqrt, rs_step = sem("rs_in"), sem("rs_sqrt"), sem("rs_step")
        vec_col, vec_turned, vec_stored, vec_in = sem("vec_col"), sem("vec_turned"), sem("vec_stored"), sem("vec_in")
        mv_done = sem("mv_done")
        slot_freed, V_ready, top_ready, index_ready, weight_ready = (
            sem("slot_freed"), sem("V_ready"), sem("top_ready"), sem("index_ready"), sem("weight_ready"))
        gather_begun, term_added = sem("gather_begun"), sem("term_added")
        gather_in = [[sem(f"gather_in{i}_{j}") for j in range(KEEP)] for i in range(2)]
        out_stored = sem("out_stored")

        def T_count(m):
            return NC + 1 + m

        def stage_count(m):
            if m < LATE:
                return 16 * (GROUPS + (GROUPS + 1) * (m // 2))
            return 16 * ((GROUPS + 1) * (m - LATE + 1) + (GROUPS if m == FULL else 0))

        def lo_count(k):
            return min(k, MIX) + (k == 0)

        streamed = list(range(HEAD, NB)) + list(range(NT)) * 2
        MV1 = NB - HEAD
        MV2 = MV1 + NT
        slots = stream + [prod[:, i, :] for i in range(2)]
        slot_of = [n % len(slots) if n < MV1 else (n - MV1) % RING for n in range(len(streamed))]
        slot_of[MV2 + 6:] = [(2, 0)[n % 2] for n in range(NT - 6)]

        def occupant_before(n):
            return max((i for i in range(n) if slot_of[i] == slot_of[n]), default=None)

        def parts(n):
            k = streamed[n]
            even = LAST // G * G
            if n < MV1 and k == MIX:
                return [(0, MAIN, even), (even, MAIN + even, LAST - even), (LAST, MAIN, CUT)]
            if n < MV1 and k > MIX:
                return [(0, MAIN + CUT, LAST - CUT), (LAST - CUT, MAIN, LAST)]
            if k < FULL:
                return [(a * G, a * SPAN + k * G, G) for a in range(GROUPS)]
            return [(0, MAIN, even), (even, MAIN + even, LAST - even)]

        parts_of = [parts(n) for n in range(len(streamed))]

        def wait_streamed(engine, n):
            engine.wait_ge(stream_in[slot_of[n]], 16 * sum(len(parts_of[i]) for i in range(n + 1)
                                                           if slot_of[i] == slot_of[n]))

        def group_rows(dram, a):
            return dram[a * SPAN:(a + 1) * SPAN, :].rearrange("(k i) f -> i k f", i=G)

        def node_cells(row_of_nodes, tile):
            return row_of_nodes.rearrange("p (b c) -> p b c", b=GROUPS)[:, :, bass.ds(tile * G, G)]

        block = ctx.enter_context(nc.Block())

        @block.sync
        def _(sp):
            def load_head(m):
                for a in range(GROUPS):
                    row = a * SPAN + m * G
                    sp.dma_start(row_stage[a * G:(a + 1) * G, m, 0:N], adj[row:row + G, :]).then_inc(stage_in[m], 16)

            def load_stage(m, signal):
                if m < FULL:
                    tile = adj[0:MAIN, :].rearrange("(b k j) n -> k j b n", b=GROUPS, j=G)[m]
                    last = adj[0:MAIN, MAIN:N].rearrange("(b k j) n -> k b j n", b=GROUPS, j=G)[m]
                else:
                    tile = adj[MAIN:MAIN + LAST // G * G, :].rearrange("(b j) n -> j b n", j=G)
                    last = adj[MAIN:N, MAIN:N]
                for a in range(GROUPS):
                    staged = row_stage[a * G:(a + 1) * G, m % 2, 0:MAIN].rearrange("p (b c) -> p b c", b=GROUPS)
                    sp.dma_start(staged[:, 0:tile.shape[1], :], tile[:, :, a * SPAN:(a + 1) * SPAN]).then_inc(signal, 16)
                    if m == FULL:
                        sp.dma_start(staged[0:LAST % G, LAST // G, :],
                                     adj[N - LAST % G:N, a * SPAN:(a + 1) * SPAN]).then_inc(signal, 16)
                sp.dma_start(row_stage[0:rows(m), m % 2, MAIN:N], last).then_inc(signal, 16)

            def load_stream(n):
                old = occupant_before(n)
                if old is not None and old < MV1:
                    sp.wait_ge(lo_ready, lo_count(streamed[old]))
                elif old is not None:
                    sp.wait_ge(mv_done, old - MV1 + 1)
                for lane, row, count in parts_of[n]:
                    sp.dma_start(slots[slot_of[n]][lane:lane + count, :],
                                 adj[row:row + count, :]).then_inc(stream_in[slot_of[n]], 16)

            def store_vector(v):
                sp.wait_ge(vec_turned, v + 1)
                for q in range(4):
                    sp.dma_start(vec_cells[q], vec32T[32 * q:32 * q + NT, :]).then_inc(vec_stored, 16)

            def broadcast_vector(v):
                sp.wait_ge(vec_stored, 64 * (v + 1))
                nodes = vec_cells.rearrange("b k q -> b (k q)")[:, 0:SPAN]
                sp.dma_start(vec_bc[:, 0:MAIN].rearrange("p (b c) -> p b c", b=GROUPS),
                             nodes.partition_broadcast(P)).then_inc(vec_in, 16)
                sp.dma_start(vec_bc[:, MAIN:MAIN + 3 * G].rearrange("p (b c) -> p b c", b=3),
                             vec_cells[0:3, FULL, :].partition_broadcast(P)).then_inc(vec_in, 16)

            def load_inputs():
                sp.wait_ge(x_padded, 1)
                for a in range(GROUPS):
                    sp.dma_start(y_out[a * G:(a + 1) * G, 0:FULL, :], group_rows(x, a)).then_inc(x_in, 16)
                sp.dma_start(y_out[0:LAST, FULL, :], x[MAIN:N, :]).then_inc(x_in, 16)
                sp.dma_start(b_bc[:, :], b.partition_broadcast(P)).then_inc(small_in, 16)
                sp.dma_start(W_sb, W).then_inc(small_in, 16)

            load_head(0)
            load_head(1)
            for n in range(MV1):
                if occupant_before(n) == 0:
                    load_inputs()
                load_stream(n)
            sp.wait_ge(lo_ready, 1)
            sp.wait_ge(tile1_low, 1)
            sp.wait_ge(T_made, T_count(1))
            load_stage(2, stage_in[0])
            load_stream(MV1)
            load_stage(3, stage_in[1])
            store_vector(0)
            load_stream(MV1 + 1)
            broadcast_vector(0)
            for n in range(MV1 + 2, MV2 + 1):
                load_stream(n)
                if n == MV1 + 5:
                    sp.wait_ge(T_made, T_count(2))
                    load_stage(4, stage_in[0])
                if n == MV1 + 8:
                    sp.wait_ge(T_made, T_count(3))
                    load_stage(5, stage_in[1])
            store_vector(1)
            load_stream(MV2 + 1)
            broadcast_vector(1)
            for n in range(MV2 + 2, len(streamed)):
                load_stream(n)
                if n == MV2 + 6:
                    sp.wait_ge(T_made, T_count(4))
                    load_stage(6, stage_in[0])
            sp.wait_ge(T_made, T_count(5))
            load_stage(LATE, late_stage_in)
            store_vector(2)
            broadcast_vector(2)
            for m in range(LATE + 1, NT):
                sp.wait_ge(late_stage_in, stage_count(m - 1))
                sp.wait_ge(T_made, T_count(m - 2))
                load_stage(m, late_stage_in)
            sp.wait_ge(term_added, KEEP * FULL)
            for a in range(GROUPS):
                sp.dma_start(group_rows(out, a), y_out[a * G:(a + 1) * G, 0:FULL, :]).then_inc(out_stored, 16)
            sp.wait_ge(term_added, KEEP * NT)
            sp.dma_start(out[FULL * P:N, :], y_out[0:LAST, FULL, :]).then_inc(out_stored, 16)
            sp.wait_ge(out_stored, 16 * (GROUPS + 1))

        @block.gpsimd
        def _(pool):
            nc.gpsimd.memset(y_out[:, FULL, :], 0.0).then_inc(x_padded, 1)
            nc.gpsimd.memset(ident[:, :], 0.0).then_inc(ident_zero, 1)
            pool.wait_ge(ident_zero, 1)
            nc.gpsimd.affine_select(out=ident[:, :], in_=ident[:, :], compare_op=ALU.not_equal, fill=1.0,
                                    base=0, pattern=[[-1, P]], channel_multiplier=1).then_inc(ident_ready, 1)
            nc.gpsimd.memset(low_of_L[:, :], 0.0).then_inc(mix_step, 1)
            nc.gpsimd.memset(sign_of_A[:, :], 1.0).then_inc(mix_step, 1)
            nc.gpsimd.memset(low_of_A[:, :], 1.0).then_inc(mix_step, 1)
            pool.wait_ge(mix_step, 3)
            masks = [(low_of_L[:, 0:1], -1.0, LAST, -1), (low_of_L[:, 1:2], -1.0, CUT - LAST + 1, 1),
                     (sign_of_A[:, :], -1.0, LAST, -1), (low_of_A[:, :], 0.0, CUT - LAST + 1, 1)]
            for mask, fill, base, step in masks:
                nc.gpsimd.affine_select(out=mask, in_=mask, compare_op=ALU.is_gt, fill=fill, base=base,
                                        pattern=[[0, 1]], channel_multiplier=step).then_inc(masks_ready, 1)

            def gather_blocks(m, piece):
                k0, k1 = piece[0], min(piece[-1] + 1, MIX)
                nc.gpsimd.tensor_copy(
                    in_blocks[m][:, k0 * P:k1 * P].rearrange("p (k b i) -> p k b i", b=GROUPS, i=G),
                    row_stage[:, m, 0:MAIN].rearrange("p (b k i) -> p k b i", b=GROUPS, i=G)[:, k0:k1]
                    ).then_inc(head_blocks, 1)

            for m in range(HEAD):
                pool.wait_ge(stage_in[m], stage_count(m))
                gather_blocks(m, PIECES[0])
            for m in range(HEAD):
                gather_blocks(m, PIECES[1])
            pool.wait_ge(hi_ready, 2)
            nc.gpsimd.tensor_tensor(A_lo[:, 1, :], row_stage[:, 1, 0:N], A_hi[:, 1, :].bitcast(f32),
                                    ALU.subtract).then_inc(tile1_low, 1)
            for piece in PIECES[2:]:
                for m in range(HEAD):
                    gather_blocks(m, piece)
            for m in range(HEAD):
                nc.gpsimd.tensor_copy(row_stage[:, m, N:NS].rearrange("p (a q) -> p a q", a=2),
                                      row_stage[:, m, MAIN:N].unsqueeze(1).to_broadcast([P, 2, LAST])
                                      ).then_inc(head_again, 1)
            pool.wait_ge(x_in, 16 * (GROUPS + 1))
            mean_bc = mean[:, :].unsqueeze(2).to_broadcast([P, NT, F])
            rstd_bc = rstd[:, :].unsqueeze(2).to_broadcast([P, NT, F])
            pool.wait_ge(ln_mean, 1)
            nc.gpsimd.tensor_tensor(xc, y_out[:, :, :], mean_bc, ALU.subtract).then_inc(ln_step, 1)
            pool.wait_ge(ln_step, 1)
            nc.gpsimd.tensor_tensor(h[:, :, :], xc, xc, ALU.mult).then_inc(ln_centered, 1)
            nc.gpsimd.tensor_scalar(xc, xc, 0.0, None, ALU.max).then_inc(ln_step, 1)
            pool.wait_ge(small_in, 32)
            nc.gpsimd.tensor_tensor(y_out[:, :, :], y_out[:, :, :],
                                    b_bc[:, :].unsqueeze(1).to_broadcast([P, NT, F]), ALU.add).then_inc(xb_ready, 1)
            pool.wait_ge(ln_step, 2)
            pool.wait_ge(ln_rstd, 1)
            nc.gpsimd.tensor_tensor(h[:, :, :], xc, rstd_bc, ALU.mult).then_inc(h_ready, 1)
            pool.wait_ge(g_copied, 1)
            for a in range(GROUPS):
                pool.dma_start(group_rows(g_dram, a), h[a * G:(a + 1) * G, 0:FULL, :]).then_inc(g_stored, 16)
            pool.dma_start(g_dram[FULL * P:N, :], h[0:LAST, FULL, :]).then_inc(g_stored, 16)
            pool.wait_ge(g_stored, 16 * (GROUPS + 1))
            nc.gpsimd.memset(mix_ident, 0.0).then_inc(mix_step, 1)
            for i, (block, shift) in enumerate([(0, 0), (0, -LAST), (1, CUT), (1, CUT - LAST)]):
                pool.wait_ge(mix_step, 4 + i)
                half = mix_ident[:, block * P:(block + 1) * P]
                nc.gpsimd.affine_select(out=half, in_=half, compare_op=ALU.not_equal, fill=1.0, base=shift,
                                        pattern=[[-1, P]], channel_multiplier=1).then_inc(mix_step, 1)
            pool.wait_ge(mix_step, 8)
            pool.sem_inc(mix_ident_ready, 1)
            def gather(q, nr):
                for j in range(KEEP):
                    nc.gpsimd.indirect_dma_start(
                        gathered[q][0:nr, j, :], None, g_dram[:, :],
                        bass.IndirectOffsetOnAxis(ap=index[0:nr, q, j:j + 1], axis=0)).then_inc(gather_in[q][j], 16)

            with pool.Fori(0, FULL // 2) as pair:
                for q in range(2):
                    pool.wait_ge(index_ready, 2 * pair + (q + 1))
                    pool.sem_inc(gather_begun, 1)
                    gather(q, P)
            pool.wait_ge(index_ready, NT)
            gather(FULL % 2, LAST)

        @block.scalar
        def _(act):
            act.dma_start(th[:, :], theta.partition_broadcast(P)).then_inc(theta_in, 16)
            act.wait_ge(theta_in, 16)
            nc.scalar.activation(t[:, :], th[:, :], ACT.Exp, scale=-1.0).then_inc(th_exp, 1)

            def row_sum(k):
                if k < HEAD:
                    act.wait_ge(stage_in[k], stage_count(k))
                    src = row_stage[:, k, 0:N]
                else:
                    wait_streamed(act, k - HEAD)
                    src = slots[slot_of[k - HEAD]][0:lanes(k), :]
                if k:
                    act.wait_ge(deg_ready, k)
                nc.scalar.activation(act_junk[0:lanes(k), :], src, ACT.Copy,
                                     accum_out=deg[0:lanes(k), k:k + 1]).then_inc(deg_ready, 1)

            def head_scale(k, m0, m1, count):
                kr = lanes(k)
                nc.scalar.activation(head_LT[0:kr, k % 4, m0:m1, :], T[0:kr, m0:m1, (k % 4) * P:(k % 4 + 1) * P],
                                     ACT.Copy, scale=s[0:kr, k:k + 1]).then_inc(hd_scaled, 1)
                act.wait_ge(hd_scaled, count)

            def head_high(k, m0, m1):
                kr = lanes(k)
                nc.scalar.activation(L_hi[0:kr, m0:m1, k * P:(k + 1) * P], head_LT[0:kr, k % 4, m0:m1, :],
                                     ACT.Copy).then_inc(hd_Lhi, 1)

            def scale_main(main, blocks=range(MIX)):
                for k in blocks:
                    block = main[:, k * P:(k + 1) * P]
                    ins = nc.scalar.activation(block, block, ACT.Copy, scale=s[:, k:k + 1])
                return ins

            act.wait_ge(cleared, 1)
            row_sum(0)
            act.wait_ge(T_made, 1)
            act.wait_ge(s_ready, 1)
            head_scale(0, 0, 1, 1)
            act.wait_ge(hd_diag, 1)
            head_high(0, 0, 1)
            act.wait_ge(T_made, 2)
            head_scale(0, 1, 2, 2)
            head_high(0, 1, 2)
            row_sum(1)
            for k in range(1, NB):
                if k == 1 or k % 4 == 0:
                    act.wait_ge(T_made, k // 4 + 3)
                for i in {1: (), 2: (3,), 3: (4, 5), 4: (6, 7)}.get(k, (k + 3,)):
                    if i < NB:
                        row_sum(i)
                if k >= MIX:
                    act.wait_ge(LT_turned, 1)
                    half = range(MIX // 2) if k == MIX else range(MIX // 2, MIX)
                    scale_main(LT2, half).then_inc(LT2_scaled, 1)
                act.wait_ge(s_ready, k + 1)
                if k >= 4:
                    act.wait_ge(hd_Llo, k - 2)
                head_scale(k, 0, 2, k + 2)
                if k < HEAD:
                    act.wait_ge(hd_diag, k + 1)
                if k % 4 == 3:
                    act.sem_inc(T_used, 1)
                head_high(k, 0, 2)
                if k == 1:
                    row_sum(2)
                if k == NT - 3:
                    act.wait_ge(deg_ready, NB)
                    nc.scalar.activation(D[:, :], deg[:, 0:NT], ACT.Sqrt).then_inc(rs_sqrt, 1)

            def scale_mixed(bank):
                for k in (MIX, MIX + 1):
                    ins = nc.scalar.activation(LT[0:lanes(k), k * P:(k + 1) * P],
                                               T[0:lanes(k), bank, (k - MIX) * P:(k - MIX + 1) * P],
                                               ACT.Copy, scale=s[0:lanes(k), k:k + 1])
                return ins

            def scale_tile(m, p):
                act.wait_ge(LT_turned, m - 1)
                scale_main(LT)
                act.wait_ge(T_made, T_count(m))
                scale_mixed(p).then_inc(LT_scaled, 1)

            def high_tile(m, p):
                act.wait_ge(LT_ready, m - 1)
                act.wait_ge(U_done, m - 1)
                nc.scalar.activation(L_hi[:, p, :], LT[:, :], ACT.Copy).then_inc(Lhi_ready, 1)

            def copy_product(m, p, slot):
                act.wait_ge(U_done, m + 1)
                nc.scalar.activation(prod_flat[:, bass.ds(slot * N, N)],
                                     U[p][:, 0:N], ACT.Copy).then_inc(U_copied, 1)

            act.wait_ge(T_made, T_count(2))
            scale_mixed(0).then_inc(LT_scaled, 1)
            act.wait_ge(LT_ready, 1)
            for c in range(NC):
                if c == 1:
                    copy_product(0, 0, 0)
                if c == NC - 1:
                    act.wait_ge(LT_scaled, 1)
                    nc.scalar.activation(L_hi[:, 0, MAIN:NP], LT[:, MAIN:NP], ACT.Copy)
                cols = slice(BLK[c][0] * P, min(BLK[c][-1] + 1, MIX) * P)
                nc.scalar.activation(L_hi[:, 0, cols], LT2[:, cols], ACT.Copy).then_inc(Lhi_ready, 1)
            act.wait_ge(ln_sqrt_in, 1)
            nc.scalar.activation(rstd[:, :], mean[:, :], ACT.Sqrt).then_inc(ln_sqrt, 1)
            copy_product(1, 1, 1)
            scale_tile(3, 1)
            act.wait_ge(hT_made, 1)
            nc.scalar.activation(hT, hT_ps, ACT.Copy).then_inc(hT_copied, 1)
            nc.scalar.activation(WT_sb[:, :], WT_ps, ACT.Copy).then_inc(hT_copied, 1)
            high_tile(3, 1)
            act.wait_ge(g_made, 1)
            nc.scalar.activation(h[:, :, :], g_ps, ACT.Copy).then_inc(g_copied, 1)
            scale_tile(4, 0)
            high_tile(4, 0)
            copy_product(2, 0, 2)
            scale_tile(5, 1)

            high_tile(5, 1)
            act.wait_ge(slot_freed, 1)
            copy_product(3, 1, 3)
            scale_tile(6, 0)
            act.wait_ge(rs_in, 1)
            nc.scalar.activation(w[:, :], deg2[:, :], ACT.Sqrt).then_inc(rs_sqrt, 1)
            high_tile(6, 0)
            copy_product(4, 0, 4)

            def step(m, p):
                act.wait_ge(LT_turned, m)
                scale_main(LT)
                act.wait_ge(slot_freed, m - (XR - 1))
                copy_product(m - 1, 1 - p, (m - 1) % XR)
                act.wait_ge(T_made, T_count(m + 1))
                scale_mixed(1 - p).then_inc(LT_scaled, 1)
                high_tile(m + 1, 1 - p)

            with act.Fori(3, FULL // 2) as pair:
                step(2 * pair, 0)
                step(2 * pair + 1, 1)
            act.wait_ge(slot_freed, FULL - (XR - 1))
            copy_product(FULL - 1, 1, (FULL - 1) % XR)

        @block.vector
        def _(dve):
            v = nc.vector

            def rsqrt_newton(dst, src, step_sem, base):
                v.reciprocal(dst, dst).then_inc(step_sem, 1)
                dve.wait_ge(step_sem, base + 1)
                v.tensor_tensor(tmp[:, :], dst, dst, ALU.mult).then_inc(step_sem, 1)
                dve.wait_ge(step_sem, base + 2)
                v.tensor_tensor(tmp[:, :], tmp[:, :], src, ALU.mult).then_inc(step_sem, 1)
                dve.wait_ge(step_sem, base + 3)
                v.tensor_scalar(tmp[:, :], tmp[:, :], -0.5, 1.5, ALU.mult, ALU.add).then_inc(step_sem, 1)
                dve.wait_ge(step_sem, base + 4)
                v.tensor_tensor(dst, dst, tmp[:, :], ALU.mult).then_inc(step_sem, 1)
                dve.wait_ge(step_sem, base + 5)

            v.memset(vec32[:, :], 0.0)
            v.memset(yv[:, :], 0.0)
            v.memset(zv[:, :], 0.0)
            v.memset(LT[:, NT * P:NP], 0.0)
            v.memset(deg[:, :], 1.0).then_inc(cleared, 1)

            dve.wait_ge(th_exp, 1)
            v.tensor_scalar_add(t[:, :], t[:, :], 1.0).then_inc(t_part, 1)
            dve.wait_ge(t_part, 1)
            v.reciprocal(t[:, :], t[:, :]).then_inc(t_ready, 1)
            dve.wait_ge(t_ready, 1)
            dve.wait_ge(ident_ready, 1)
            v.tensor_scalar(t0_ident[:, :], ident[:, :], t[:, 0:1], None, ALU.mult).then_inc(t0i_ready, 1)

            def source(k):
                return row_stage[:, k, 0:N] if k < HEAD else slots[slot_of[k - HEAD]][0:lanes(k), :]

            def high(k):
                if k < HEAD:
                    dve.wait_ge(stage_in[k], stage_count(k))
                else:
                    wait_streamed(dve, k - HEAD)
                if k < MIX:
                    v.tensor_copy(A_hi[:, k, :], source(k)).then_inc(hi_ready, 1)
                elif k == MIX:
                    dve.wait_ge(masks_ready, 4)
                    v.tensor_scalar(A_hi[:, k, :], source(k), sign_of_A[:, :], None, ALU.mult).then_inc(hi_ready, 1)
                else:
                    v.tensor_copy(A_lo[0:lanes(k), MIX, :], source(k)).then_inc(hi_ready, 1)

            def low(k):
                dve.wait_ge(hi_ready, k + 1)
                if k < MIX:
                    v.tensor_tensor(A_lo[:, k, :], source(k), A_hi[:, k, :].bitcast(f32),
                                    ALU.subtract).then_inc(lo_ready, 1)
                elif k > MIX:
                    kr = lanes(k)
                    v.scalar_tensor_tensor(A_lo[0:kr, MIX, :], source(k), low_of_A[0:kr, :],
                                           A_lo[0:kr, MIX, :].bitcast(f32), ALU.mult,
                                           ALU.subtract).then_inc(lo_ready, 1)

            def scale_of(k):
                dve.wait_ge(deg_ready, k + 1)
                v.reciprocal(rdeg[:, k:k + 1], deg[:, k:k + 1]).then_inc(rdeg_ready, 1)
                dve.wait_ge(rdeg_ready, k + 1)
                v.tensor_scalar(s[:, k:k + 1], rdeg[:, k:k + 1], t[:, 1:2], None, ALU.mult).then_inc(s_ready, 1)

            def head_diagonal(k, count):
                dve.wait_ge(hd_scaled, count)
                v.tensor_tensor(head_LT[:, k, k, :], head_LT[:, k, k, :], t0_ident[:, :], ALU.add).then_inc(hd_diag, 1)

            def head_low(k, m0, m1, count):
                dve.wait_ge(hd_Lhi, count)
                kr = lanes(k)
                both = head_LT[0:kr, k % 4, m0:m1, :]
                high = L_hi[0:kr, m0:m1, k * P:(k + 1) * P]
                if k < MIX:
                    v.tensor_tensor(L_lo[0:kr, m0:m1, k * P:(k + 1) * P], both, high.bitcast(f32),
                                    ALU.subtract).then_inc(hd_Llo, 1)
                else:
                    v.scalar_tensor_tensor(high, both, low_of_L[0:kr, k - MIX:k - MIX + 1], high.bitcast(f32),
                                           ALU.mult, ALU.add).then_inc(hd_Llo, 1)

            def turn_vector(n, col):
                v.tensor_copy(vec32[:, 0:NT], col).then_inc(vec_col, 1)
                dve.wait_ge(vec_col, n + 1)
                if n >= 1:
                    dve.wait_ge(vec_stored, 64 * n)
                v.transpose(vec32T[:, :], vec32[:, :]).then_inc(vec_turned, 1)

            def turn_tile(m, p, main):
                if isinstance(m, int) and m < LATE:
                    dve.wait_ge(stage_in[p], stage_count(m))
                else:
                    dve.wait_ge(late_stage_in, stage_count(m))
                v.transpose(main[:, 0:MAIN].rearrange("p (k b j) -> p b k j", b=GROUPS, j=G),
                            row_stage_flat[:, bass.ds(p * NS, MAIN)].rearrange("p (b k i) -> p b k i", b=GROUPS, i=G)
                            ).then_inc(LT_turned, 1)
                v.tensor_copy(row_stage_flat[:, bass.ds(p * NS + N, 2 * LAST)].rearrange("p (a q) -> p a q", a=2),
                              row_stage_flat[:, bass.ds(p * NS + MAIN, LAST)].unsqueeze(1).to_broadcast([P, 2, LAST])
                              ).then_inc(again_ready, 1)

            row_stage_flat = row_stage[:, :, :].rearrange("p a n -> p (a n)")
            dve.wait_ge(t0i_ready, 1)
            high(0)
            scale_of(0)
            head_diagonal(0, 1)
            low(0)
            head_low(0, 0, 1, 1)
            head_low(0, 1, 2, 2)
            high(1)
            scale_of(1)
            head_diagonal(1, 3)
            head_low(1, 0, 2, 3)
            high(2)
            scale_of(2)
            low(2)
            for k in range(2, NB):
                if k + 1 < NB:
                    high(k + 1)
                    scale_of(k + 1)
                head_low(k, 0, 2, k + 2)
                if k + 1 < NB:
                    low(k + 1)
                if k == NT - 3:
                    dve.wait_ge(rs_sqrt, 1)
                    rsqrt_newton(D[:, :], deg[:, 0:NT], rs_step, 0)
                    turn_vector(0, D[:, :])
                    turn_tile(2, 0, LT2)
            dve.wait_ge(x_in, 16 * (GROUPS + 1))
            v.reduce_sum(mean[:, :], y_out[:, :, :], AX.X).then_inc(ln_sum, 1)
            dve.wait_ge(ln_sum, 1)
            v.tensor_scalar(mean[:, :], mean[:, :], 1.0 / F, None, ALU.mult).then_inc(ln_mean, 1)

            def add_diagonal(m):
                dve.wait_ge(LT_scaled, m - 1)
                v.tensor_tensor(LT[:, bass.ds(m * P, P)], LT[:, bass.ds(m * P, P)], t0_ident[:, :],
                                ALU.add).then_inc(LT_ready, 1)

            def add_last_diagonal():
                dve.wait_ge(LT_scaled, FULL - 1)
                dve.wait_ge(mix_ident_ready, 1)
                v.scalar_tensor_tensor(LT[:, MIX * P:NP], mix_ident, t[:, 0:1], LT[:, MIX * P:NP],
                                       ALU.mult, ALU.add).then_inc(LT_ready, 1)

            def mix_L(p):
                for k in (MIX, MIX + 1):
                    block = L_hi_flat[:, bass.ds(p * NP + k * P, P)]
                    ins = v.scalar_tensor_tensor(block, LT[:, k * P:(k + 1) * P], low_of_L[:, k - MIX:k - MIX + 1],
                                                 block.bitcast(f32), ALU.mult, ALU.add)
                return ins

            def low_L(m, p):
                dve.wait_ge(Lhi_ready, m - 2 + NC)
                v.tensor_tensor(L_lo_flat[:, bass.ds(p * (MIX * P), MIX * P)], LT[:, 0:MIX * P],
                                L_hi_flat[:, bass.ds(p * NP, MIX * P)].bitcast(f32), ALU.subtract)
                mix_L(p).then_inc(Llo_ready, 1)

            def low_L2(c):
                dve.wait_ge(Lhi_ready, c + 1)
                cols = slice(BLK[c][0] * P, min(BLK[c][-1] + 1, MIX) * P)
                ins = v.tensor_tensor(L_lo[:, 0, cols], LT2[:, cols], L_hi[:, 0, cols].bitcast(f32), ALU.subtract)
                if c == NC - 1:
                    ins = mix_L(0)
                ins.then_inc(Llo_ready, 1)

            def turn_next(m, p):
                dve.wait_ge(Llo_ready, m - 3 + NC)
                turn_tile(m, p, LT)

            L_lo_flat = L_lo[:, :, :].rearrange("p a n -> p (a n)")
            L_hi_flat = L_hi[:, :, :].rearrange("p a n -> p (a n)")

            last_in_middle = max(n for n in range(len(streamed)) if slot_of[n] == 1)

            def times_vector(n, dst, k0, k1):
                dve.wait_ge(vec_in, 32 * (n + 1))
                for k in range(k0, k1):
                    i = (MV1, MV2)[n] + k
                    wait_streamed(dve, i)
                    if NT * n + k:
                        dve.wait_ge(mv_done, NT * n + k)
                    if i - 1 == last_in_middle:
                        dve.sem_inc(slot_freed, 1)
                    v.tensor_tensor_reduce(out=V[0:rows(k), 0:N], in0=slots[slot_of[i]][0:rows(k), :],
                                           in1=vec_bc[0:rows(k), 0:N], scale=1.0, scalar=0.0,
                                           op0=ALU.mult, op1=ALU.add,
                                           accum_out=dst[0:rows(k), k:k + 1]).then_inc(mv_done, 1)

            dve.wait_ge(LT2_scaled, 2)
            v.tensor_tensor(LT2[:, 2 * P:3 * P], LT2[:, 2 * P:3 * P], t0_ident[:, :], ALU.add).then_inc(LT_ready, 1)
            low_L2(0)
            low_L2(1)
            dve.wait_ge(ln_centered, 1)
            v.reduce_sum(mean[:, :], h[:, :, :], AX.X).then_inc(ln_var, 1)
            dve.wait_ge(ln_var, 1)
            v.tensor_scalar(mean[:, :], mean[:, :], 1.0 / F, EPS, ALU.mult, ALU.add).then_inc(ln_sqrt_in, 1)
            low_L2(2)
            dve.wait_ge(Llo_ready, NC)
            turn_tile(3, 1, LT)
            dve.wait_ge(ln_sqrt, 1)
            rsqrt_newton(rstd[:, :], mean[:, :], ln_newton, 0)
            dve.sem_inc(ln_rstd, 1)
            times_vector(0, yv, 0, 5)
            add_diagonal(3)
            times_vector(0, yv, 5, 6)
            low_L(3, 1)
            turn_next(4, 0)
            times_vector(0, yv, 6, NT)
            dve.wait_ge(mv_done, NT)
            v.tensor_tensor(tmp[:, :], s[:, 0:NT], yv[:, :], ALU.mult).then_inc(rs_step, 1)
            dve.wait_ge(rs_step, 6)
            turn_vector(1, tmp[:, :])
            add_diagonal(4)
            low_L(4, 0)
            turn_next(5, 1)
            times_vector(1, zv, 0, 6)
            add_diagonal(5)
            times_vector(1, zv, 6, 7)
            low_L(5, 1)
            turn_next(6, 0)
            times_vector(1, zv, 7, NT)
            dve.wait_ge(mv_done, 2 * NT)
            v.scalar_tensor_tensor(deg2[:, :], yv[:, :], t[:, 0:1], zv[:, :], ALU.mult, ALU.add).then_inc(rs_step, 1)
            dve.wait_ge(rs_step, 7)
            v.tensor_tensor(deg2[:, :], deg2[:, :], D[:, :], ALU.mult).then_inc(rs_step, 1)
            dve.wait_ge(rs_step, 8)
            v.tensor_scalar_add(deg2[:, :], deg2[:, :], 1.0).then_inc(rs_in, 1)
            dve.wait_ge(rs_sqrt, 2)
            rsqrt_newton(w[:, :], deg2[:, :], rs_step, 8)
            v.tensor_tensor(c_col[:, :], D[:, :], w[:, :], ALU.mult).then_inc(rs_step, 1)
            dve.wait_ge(rs_step, 14)
            v.tensor_tensor(diag[:, :], c_col[:, :], deg[:, 0:NT], ALU.mult).then_inc(rs_step, 1)
            turn_vector(2, c_col[:, :])
            add_diagonal(6)
            low_L(6, 0)
            turn_next(7, 1)
            dve.wait_ge(rs_step, 15)
            dve.wait_ge(vec_in, 96)

            def add_terms(r):
                nr, q = rows(r), r % 2
                for j in range(KEEP):
                    dve.wait_ge(gather_in[q][j], 16 * (r // 2 + 1))
                    if j:
                        dve.wait_ge(term_added, KEEP * r + j)
                    v.scalar_tensor_tensor(y_out[0:nr, r, :], gathered[q][0:nr, j, :], weight[0:nr, q, j:j + 1],
                                           y_out[0:nr, r, :], ALU.mult, ALU.add).then_inc(term_added, 1)

            def rank(r):
                q = r % 2
                dve.wait_ge(U_copied, r + 1)
                v.tensor_tensor(V[:, 0:N], prod[:, r % XR, :], vec_bc[:, 0:N], ALU.mult).then_inc(slot_freed, 1)
                dve.wait_ge(slot_freed, r + 2)
                own = node_cells(V[:, 0:MAIN], r)
                v.scalar_tensor_tensor(own, ident[:, :].rearrange("p (b j) -> p b j", j=G), diag[:, r:r + 1],
                                       own, ALU.mult, ALU.add).then_inc(V_ready, 1)
                dve.wait_ge(V_ready, r + 1)
                v.max(top[:, :], V[:, 0:N]).then_inc(top_ready, 1)
                if r >= 2:
                    add_terms(r - 2)
                    dve.wait_ge(term_added, KEEP * (r - 1))
                dve.wait_ge(top_ready, r + 1)
                v.tensor_scalar(weight[:, q, :], top[:, 0:KEEP], c_col[:, r:r + 1], None,
                                ALU.mult).then_inc(weight_ready, 1)
                v.max_index(index[:, q, :], top[:, :], V[:, 0:N]).then_inc(index_ready, 1)
                dve.wait_ge(weight_ready, r + 1)
                dve.wait_ge(index_ready, r + 1)

            def next_L(m):
                if m < FULL:
                    add_diagonal(m)
                else:
                    add_last_diagonal()
                low_L(m, m % 2)
                if m < FULL:
                    turn_next(m + 1, (m + 1) % 2)

            rank(0)
            next_L(7)
            rank(1)
            rank(2)
            next_L(8)
            rank(3)
            rank(4)
            next_L(9)
            rank(5)
            rank(6)
            next_L(10)
            rank(7)
            rank(8)
            rank(9)

            r = FULL
            for n, (c0, c1) in enumerate(CH):
                dve.wait_ge(tail_chunk, n + 1)
                v.tensor_tensor(V[0:LAST, c0:c1], U[r % 2][0:LAST, c0:c1], vec_bc[0:LAST, c0:c1],
                                ALU.mult).then_inc(slot_freed, 1)
                if n == 0:
                    add_terms(r - 2)
                if n == 1:
                    dve.wait_ge(slot_freed, r + 3)
                    v.max(top2[0:LAST, 0:8], V[0:LAST, 0:c1]).then_inc(top_ready, 1)
                    add_terms(r - 1)
            dve.wait_ge(slot_freed, r + 4)
            v.scalar_tensor_tensor(V[0:LAST, r * P:N], ident[0:LAST, 0:LAST], diag[0:LAST, r:r + 1],
                                   V[0:LAST, r * P:N], ALU.mult, ALU.add).then_inc(V_ready, 1)
            dve.wait_ge(V_ready, r + 1)
            v.max(top2[0:LAST, 8:16], V[0:LAST, CH[-1][0]:N]).then_inc(top_ready, 1)
            dve.wait_ge(top_ready, r + 2)
            v.max(top[0:LAST, :], top2[0:LAST, :]).then_inc(top_ready, 1)
            dve.wait_ge(top_ready, r + 3)
            v.max_index(index[0:LAST, r % 2, :], top[0:LAST, :], V[0:LAST, 0:N]).then_inc(index_ready, 1)
            v.tensor_scalar(weight[0:LAST, r % 2, :], top[0:LAST, 0:KEEP], c_col[0:LAST, r:r + 1], None,
                            ALU.mult).then_inc(weight_ready, 1)
            dve.wait_ge(weight_ready, r + 1)
            add_terms(r)

        @block.tensor
        def _(pe):
            mm = nc.tensor

            def transpose_piece(m_slot, piece, bank):
                for k in piece:
                    if k < MIX:
                        cols = in_blocks[m_slot][:, k * P:(k + 1) * P]
                    else:
                        cols = row_stage[:, m_slot, k * P:k * P + lanes(k)]
                    ins = mm.transpose(T[0:lanes(k), bank, (k % 4) * P:(k % 4 + 1) * P], cols, ident[:, :])
                return ins

            def transpose_mixed(p):
                for k in (MIX, MIX + 1):
                    ins = mm.transpose(T[0:lanes(k), p, (k - MIX) * P:(k - MIX + 1) * P],
                                       row_stage[:, p, k * P:k * P + lanes(k)], ident[:, :])
                return ins

            def block_one():
                for m in range(HEAD):
                    hi, lo = L_hi[:, m, P:2 * P], L_lo[:, m, P:2 * P]
                    for c0, c1 in CH:
                        mm.matmul(U[m][:, c0:c1], lo, A_hi[:, 1, c0:c1], start=False, stop=False)
                        mm.matmul(U[m][:, c0:c1], hi, A_hi[:, 1, c0:c1], start=False, stop=False)
                pe.wait_ge(tile1_low, 1)
                for m in range(HEAD):
                    for c0, c1 in CH:
                        mm.matmul(U[m][:, c0:c1], L_hi[:, m, P:2 * P], A_lo[:, 1, c0:c1], start=False, stop=False)

            def three_passes(p, k, c0, c1, cols):
                o = U[p][0:cols, c0:c1]
                if k == MIX:
                    kr = lanes(MIX + 1)
                    mm.matmul(o, L_hi[:, p, MIX * P:MIX * P + cols], A_hi[:, MIX, c0:c1], start=False, stop=False)
                    return mm.matmul(o, L_hi[0:kr, p, (MIX + 1) * P:(MIX + 1) * P + cols], A_lo[0:kr, MIX, c0:c1],
                                     start=False, stop=True)
                hi = L_hi[:, p, k * P:k * P + cols]
                lo = L_lo[:, p, k * P:k * P + cols]
                mm.matmul(o, lo, A_hi[:, k, c0:c1], start=(k == 0), stop=False)
                mm.matmul(o, hi, A_lo[:, k, c0:c1], start=False, stop=False)
                return mm.matmul(o, hi, A_hi[:, k, c0:c1], start=False, stop=False)

            def keep_busy(n):
                for _ in range(n):
                    mm.matmul(U[1][:, 0:P], ident[:, :], ident[:, :], start=True, stop=True)

            pe.wait_ge(ident_ready, 1)
            keep_busy(11)
            pe.wait_ge(head_blocks, 1)
            transpose_piece(0, PIECES[0], 0).then_inc(T_made, 1)
            keep_busy(8)
            pe.wait_ge(head_blocks, 2)
            transpose_piece(1, PIECES[0], 1).then_inc(T_made, 1)
            def first_block():
                hi, lo = L_hi[:, 0, 0:P], L_lo[:, 0, 0:P]
                pe.wait_ge(hd_Lhi, 1)
                for c0, c1 in CH:
                    mm.matmul(U[0][:, c0:c1], hi, A_hi[:, 0, c0:c1], start=True, stop=False)
                pe.wait_ge(lo_ready, 1)
                for c0, c1 in CH:
                    mm.matmul(U[0][:, c0:c1], hi, A_lo[:, 0, c0:c1], start=False, stop=False)
                pe.wait_ge(hd_Llo, 1)
                for c0, c1 in CH:
                    mm.matmul(U[0][:, c0:c1], lo, A_hi[:, 0, c0:c1], start=False, stop=False)

            for k in range(NT):
                if k == MIX:
                    pe.wait_ge(T_used, NC)
                    pe.wait_ge(again_ready, 1)
                    transpose_mixed(0).then_inc(T_made, 1)
                if k == 1:
                    pe.wait_ge(hd_Llo, 3)
                    block_one()
                    continue
                if k:
                    pe.wait_ge(lo_ready, lo_count(k))
                for m in range(HEAD):
                    if k == 0 and m == 1:
                        pe.wait_ge(hd_Llo, 2)
                    elif k == 0:
                        pass
                    elif m == 0:
                        pe.wait_ge(hd_Llo, k + 2 if k < MIX else NB + 1)
                    if (k, m) == (0, 0):
                        first_block()
                        pe.wait_ge(hd_scaled, HEAD)
                        pe.wait_ge(head_blocks, 2 * HEAD)
                        transpose_piece(0, PIECES[1], 0)
                        transpose_piece(1, PIECES[1], 1).then_inc(T_made, 1)
                    else:
                        for c0, c1 in CH:
                            ins = three_passes(m, k, c0, c1, P)
                    if k == NT - 1:
                        ins.then_inc(U_done, 1)
                    if k in (2, 6) and m == 0:
                        pe.wait_ge(T_used, k // 4 + 1)
                        pe.wait_ge(head_blocks, HEAD * (k // 4 + 3))
                        if k == 6:
                            pe.wait_ge(head_again, HEAD)
                        transpose_piece(0, BLK[k // 4 + 1], 0)
                        transpose_piece(1, BLK[k // 4 + 1], 1).then_inc(T_made, 1)

            def transpose_h():
                pe.wait_ge(U_copied, 2)
                pe.wait_ge(h_ready, 1)
                for k in range(NT):
                    mm.transpose(hT_ps[:, k * P:k * P + rows(k)], h[0:rows(k), k, :], ident[0:rows(k), 0:rows(k)])
                pe.wait_ge(small_in, 32)
                mm.transpose(WT_ps, W_sb[:, :], ident[0:F, 0:F]).then_inc(hT_made, 1)

            def multiply_h():
                pe.wait_ge(hT_copied, 2)
                for k in range(NT):
                    ins = mm.matmul(g_ps[0:rows(k), k, :], hT[:, k * P:k * P + rows(k)], WT_sb[:, :],
                                    start=True, stop=True)
                ins.then_inc(g_made, 1)

            def multiply(m, p, first=False, turn_at=(0, 2)):
                if not first:
                    pe.wait_ge(Llo_ready, m - 2 + NC)
                pe.wait_ge(U_copied, m - 1)
                for n, (c0, c1) in enumerate(CH):
                    for k in range(NT):
                        if first and n == 0 and k % 4 == 0:
                            pe.wait_ge(Llo_ready, k // 4 + 1)
                        ins = three_passes(p, k, c0, c1, P)
                        if (n, k) == turn_at:
                            pe.wait_ge(again_ready, m)
                            if not first:
                                pe.wait_ge(LT_scaled, m - 2)
                            transpose_mixed(1 - p).then_inc(T_made, 1)
                    if first and n == 0:
                        transpose_h()
                    if first and n == 1:
                        multiply_h()
                    if n == len(CH) - 1:
                        ins.then_inc(U_done, 1)

            multiply(2, 0, first=True, turn_at=(1, 0))
            pe.wait_ge(g_copied, 1)
            multiply(3, 1, turn_at=(1, 0))
            with pe.Fori(2, FULL // 2) as pair:
                multiply(2 * pair, 0)
                multiply(2 * pair + 1, 1)
            m = FULL
            pe.wait_ge(Llo_ready, m - 2 + NC)
            pe.wait_ge(U_copied, m - 1)
            for c0, c1 in CH:
                for k in range(NT):
                    ins = three_passes(m % 2, k, c0, c1, LAST)
                ins.then_inc(tail_chunk, 1)


_INS = ["x", "adj", "L0_gnn_theta", "L0_gnn_W", "L0_gnn_b"]


def kernel(**inputs):
    import numpy as _np
    import concourse.bacc as _bacc
    from concourse import mybir as _mybir
    from concourse.bass_utils import run_bass_kernel_spmd as _run

    nc = _bacc.Bacc("TRN2", target_bir_lowering=False, num_devices=1)
    arrays, args = {}, []
    for name in _INS:
        a = _np.ascontiguousarray(inputs[name])
        arrays[f"in_{name}_dram"] = a
        args.append(nc.dram_tensor(f"in_{name}_dram", a.shape, _mybir.dt.from_np(a.dtype), kind="ExternalInput").ap())
    out = nc.dram_tensor("out_dram", arrays["in_x_dram"].shape, _mybir.dt.float32, kind="ExternalOutput").ap()
    poly_graph_kernel(nc, *args, out)
    r = _run(nc, [arrays], core_ids=[0])
    return r.results[0]["out_dram"]
```
